# Optimizing a Trainium2 kernel written in Bass

```python
import numpy as np
import jax
import jax.numpy as jnp

def _softmax(x, axis=-1):
    return jax.nn.softmax(x, axis=axis)

def _gelu(x):
    return jax.nn.gelu(x, approximate=True)

def _silu(x):
    return jax.nn.silu(x)

def _sigmoid(x):
    return jax.nn.sigmoid(x)

def _layernorm(x, axis=-1, eps=1e-05):
    m = jnp.mean(x, axis=axis, keepdims=True)
    v = jnp.var(x, axis=axis, keepdims=True)
    return (x - m) / jnp.sqrt(v + eps)

def _scatter_add(tgt, idx, src, axis=0):
    return tgt.at[idx].add(src)

def _segment_sum(src, seg, n):
    return jax.ops.segment_sum(src, seg, n)
kernel_name = 'mk_seq_preln_d1_jaxref_r4_509993'

def setup_inputs(seed: int=0):
    np.random.seed(seed)
    _w = jnp.asarray

    def _L0_attn_setup():
        import jax, jax.numpy as jnp
        import numpy as np
        DIM = 256
        HEADS = 16
        HEAD_DIM = DIM // HEADS

        def apply_rope(x):
            B, S, H, D = x.shape
            half = D // 2
            freqs = 1.0 / 10000.0 ** (jnp.arange(half, dtype=jnp.float32) / half)
            pos = jnp.arange(S, dtype=jnp.float32)
            angles = pos[:, None] * freqs[None, :]
            sin = jnp.sin(angles)[None, :, None, :]
            cos = jnp.cos(angles)[None, :, None, :]
            x1, x2 = (x[..., :half], x[..., half:])
            return jnp.concatenate([x1 * cos - x2 * sin, x1 * sin + x2 * cos], axis=-1)
        key = jax.random.key(seed)
        ks = jax.random.split(key, 5)
        x = jax.random.normal(ks[0], (2, 512, DIM), dtype=jnp.float32)
        s = 1.0 / np.sqrt(DIM)
        qkv_w = jax.random.uniform(ks[1], (3 * DIM, DIM), minval=-s, maxval=s, dtype=jnp.float32)
        qkv_b = jax.random.uniform(ks[2], (3 * DIM,), minval=-s, maxval=s, dtype=jnp.float32)
        proj_w = jax.random.uniform(ks[3], (DIM, DIM), minval=-s, maxval=s, dtype=jnp.float32)
        proj_b = jax.random.uniform(ks[4], (DIM,), minval=-s, maxval=s, dtype=jnp.float32)
        return {'x': x, 'qkv_w': qkv_w, 'qkv_b': qkv_b, 'proj_w': proj_w, 'proj_b': proj_b}
    _L0_attn_in = _L0_attn_setup()

    def _L0_ffn_setup():
        import jax, jax.numpy as jnp
        import numpy as np
        E, D, F = (8, 256, 1024)
        B, S = (4, 512)

        def _layernorm(x, g, b, eps=1e-05):
            mu = jnp.mean(x, axis=-1, keepdims=True)
            var = jnp.var(x, axis=-1, keepdims=True)
            return (x - mu) * jax.lax.rsqrt(var + eps) * g + b
        key = jax.random.key(seed)
        ks = jax.random.split(key, 5)
        return {'input_features': jax.random.normal(ks[0], (B, S, D), jnp.float32), 'centroids': jax.random.normal(ks[1], (E, D), jnp.float32) * 0.1, 'ln_g': jnp.ones((E, D), jnp.float32), 'ln_b': jnp.zeros((E, D), jnp.float32), 'w1': jax.random.normal(ks[2], (E, F, D), jnp.float32) * (1.0 / np.sqrt(D).astype(np.float32)), 'b1': jnp.zeros((E, F), jnp.float32), 'w2': jax.random.normal(ks[3], (E, D, F), jnp.float32) * (1.0 / np.sqrt(F).astype(np.float32)), 'b2': jnp.zeros((E, D), jnp.float32)}
    _L0_ffn_in = _L0_ffn_setup()
    _d = {'L0_attn_x': _L0_attn_in['x'], 'L0_attn_qkv_w': _L0_attn_in['qkv_w'], 'L0_attn_qkv_b': _L0_attn_in['qkv_b'], 'L0_attn_proj_w': _L0_attn_in['proj_w'], 'L0_attn_proj_b': _L0_attn_in['proj_b'], 'L0_ffn_centroids': _L0_ffn_in['centroids'], 'L0_ffn_ln_g': _L0_ffn_in['ln_g'], 'L0_ffn_ln_b': _L0_ffn_in['ln_b'], 'L0_ffn_w1': _L0_ffn_in['w1'], 'L0_ffn_b1': _L0_ffn_in['b1'], 'L0_ffn_w2': _L0_ffn_in['w2'], 'L0_ffn_b2': _L0_ffn_in['b2']}
    _x0 = _d['L0_attn_x']
    _d['L0_attn_x'] = jax.random.normal(jax.random.fold_in(jax.random.key(seed), 1), (4, 1024, 256), dtype=_x0.dtype)
    del _x0
    return _d

def reference(L0_attn_x, L0_attn_qkv_w, L0_attn_qkv_b, L0_attn_proj_w, L0_attn_proj_b, L0_ffn_centroids, L0_ffn_ln_g, L0_ffn_ln_b, L0_ffn_w1, L0_ffn_b1, L0_ffn_w2, L0_ffn_b2):

    def _L0_attn_ref(x, qkv_w, qkv_b, proj_w, proj_b):
        import jax, jax.numpy as jnp
        import numpy as np
        DIM = 256
        HEADS = 16
        HEAD_DIM = DIM // HEADS

        def apply_rope(x):
            B, S, H, D = x.shape
            half = D // 2
            freqs = 1.0 / 10000.0 ** (jnp.arange(half, dtype=jnp.float32) / half)
            pos = jnp.arange(S, dtype=jnp.float32)
            angles = pos[:, None] * freqs[None, :]
            sin = jnp.sin(angles)[None, :, None, :]
            cos = jnp.cos(angles)[None, :, None, :]
            x1, x2 = (x[..., :half], x[..., half:])
            return jnp.concatenate([x1 * cos - x2 * sin, x1 * sin + x2 * cos], axis=-1)
        B, S, D = x.shape
        qkv = x @ qkv_w.T + qkv_b
        q, k, v = jnp.split(qkv, 3, axis=-1)
        q = q.reshape(B, S, HEADS, HEAD_DIM)
        k = k.reshape(B, S, HEADS, HEAD_DIM)
        v = v.reshape(B, S, HEADS, HEAD_DIM)
        q = apply_rope(q)
        k = apply_rope(k)
        scale = 1.0 / np.sqrt(HEAD_DIM)
        attn = jnp.einsum('bqhd,bkhd->bhqk', q, k) * scale
        mask = jnp.triu(jnp.ones((S, S), dtype=bool), k=1)
        attn = jnp.where(mask[None, None], -1000000000.0, attn)
        attn = jax.nn.softmax(attn, axis=-1)
        out = jnp.einsum('bhqk,bkhd->bqhd', attn, v).reshape(B, S, D)
        return out @ proj_w.T + proj_b

    def _L0_ffn_ref(input_features, centroids, ln_g, ln_b, w1, b1, w2, b2):
        import jax, jax.numpy as jnp
        import numpy as np
        E, D, F = (8, 256, 1024)
        B, S = (4, 512)

        def _layernorm(x, g, b, eps=1e-05):
            mu = jnp.mean(x, axis=-1, keepdims=True)
            var = jnp.var(x, axis=-1, keepdims=True)
            return (x - mu) * jax.lax.rsqrt(var + eps) * g + b
        Bf, Sf, Df = input_features.shape
        x = input_features.reshape(-1, Df)
        aff = x @ centroids.T
        assign = jnp.argmax(aff, axis=1)
        order = jnp.argsort(assign)
        xs = x[order]
        es = assign[order]
        alpha = jax.nn.sigmoid(jnp.take_along_axis(aff[order], es[:, None], axis=1))
        nE = centroids.shape[0]
        y = jnp.zeros_like(xs)
        for e in range(nE):
            h = _layernorm(xs, ln_g[e], ln_b[e])
            h = jax.nn.relu(h @ w1[e].T + b1[e])
            ye = xs + h @ w2[e].T + b2[e]
            y = y + jnp.where((es == e)[:, None], ye, 0.0)
        out_sorted = alpha * y + (1.0 - alpha) * xs
        inv = jnp.argsort(order)
        return out_sorted[inv].reshape(Bf, Sf, Df)
    x = L0_attn_x
    x = x + _L0_attn_ref(_layernorm(x, axis=-1), L0_attn_qkv_w, L0_attn_qkv_b, L0_attn_proj_w, L0_attn_proj_b)
    x = x + _L0_ffn_ref(_layernorm(x, axis=-1), L0_ffn_centroids, L0_ffn_ln_g, L0_ffn_ln_b, L0_ffn_w1, L0_ffn_b1, L0_ffn_w2, L0_ffn_b2)
    return x

_drawn_inputs = setup_inputs


def setup_inputs(seed=0):
    import zlib

    import numpy as np

    out = dict(_drawn_inputs(seed))
    spreads = {'L0_ffn_ln_g': (1.0, 0.2),
     'L0_ffn_ln_b': (0.0, 0.272),
     'L0_ffn_b1': (0.0, 0.268),
     'L0_ffn_b2': (0.0, 0.1)}
    factors = {}
    for name, (base, spread) in spreads.items():
        noise = np.random.default_rng([zlib.crc32(name.encode()), seed]).standard_normal(out[name].shape)
        drawn = base * np.exp(spread * noise) if base else spread * noise
        out[name] = jnp.asarray(drawn.astype(out[name].dtype))
    for name, factor in factors.items():
        out[name] = (out[name] * factor).astype(out[name].dtype)
    return out
```

```python
import concourse.bass as bass
from concourse import mybir
from contextlib import ExitStack

F32 = mybir.dt.float32
BF16 = mybir.dt.bfloat16
I32 = mybir.dt.int32
U32 = mybir.dt.uint32
ALU = mybir.AluOpType
ACT = mybir.ActivationFunctionType
AX = mybir.AxisListType

P = 128
BATCH, SEQ, DIM = 4, 1024, 256
HEADS, HD = 16, 16
NTOK = BATCH * SEQ
NT = NTOK // P
DC = DIM // P
NE, FF = 8, 1024
FC = FF // P
QH = 4
QB = HEADS // QH
NQ = BATCH * QB
KB = SEQ // P
QW = 512
NSPLIT = 3
SROWS = 6 * HD
MROWS = 3
NEG = -1.0e30
EPS = 1e-5
NSLOT = (NTOK + NE * (P - 1)) // P
REGION = NTOK + P
DUMMY_ROW = NE * REGION
PAYW = 2 * DIM + 2
WCOLS = DC * FF + FC * DIM
EARLY = 5

C_ID, C_MASK, C_LT, C_IOTA, C_RIOTA, C_IOTAP, C_BLK, C_SLOT, C_ID32, C_END = (
    0, 128, 640, 768, 776, 784, 785, 817, 856, 888)


class Step:

    def __init__(self, const, reg=None, unroll=1):
        self.const, self.reg, self.unroll = const, reg, unroll

    def __add__(self, k):
        return Step(self.const + k, self.reg, self.unroll)

    def value(self):
        return self.const if self.reg is None else self.reg * self.unroll + self.const

    def within(self, total):
        return self.reg is not None or 0 <= self.const < total

    def ring(self, n):
        assert self.reg is None or self.unroll % n == 0
        return self.const % n


def run_steps(eng, emit, first, lo, hi, last, unroll):
    for n in range(first, lo):
        emit(Step(n))
    assert (hi - lo) % unroll == 0
    with eng.Fori(0, (hi - lo) // unroll) as reg:
        for u in range(unroll):
            emit(Step(lo + u, reg, unroll))
    for n in range(hi, last):
        emit(Step(n))


def wait(eng, sem, step, per=1, plus=0, alone=None):
    if step.reg is None:
        if per * step.const + plus > 0:
            eng.wait_ge(sem, per * step.const + plus)
    else:
        assert per * step.const + plus > 0
        eng.wait_ge(sem, step.reg * (per * step.unroll) + (per * step.const + plus))
        if alone is not None:
            eng.sem_inc(alone, 1)


def wait_dma(eng, sems, step, count=1, alone=None):
    n = len(sems)
    slot = step.ring(n)
    if step.reg is None:
        eng.wait_ge(sems[slot], 16 * count * (step.const // n + 1))
    else:
        eng.wait_ge(sems[slot], step.reg * (16 * count * step.unroll // n) + 16 * count * (step.const // n + 1))
        if alone is not None:
            eng.sem_inc(alone, 1)


def program(nc, x, w_qkv, b_qkv, w_proj, b_proj, cent, w_exp, cols, b2, consts, rope, out):
    ctx = ExitStack()
    with ctx:
        def sem(name):
            return ctx.enter_context(nc.semaphore(name))

        def dram(name, shape, dt):
            return nc.dram_tensor(name, shape, dt, kind="Internal").ap()

        parts_d = dram("qk_parts", [2, NSPLIT, DIM, NTOK], BF16)
        att_d = dram("attention", [NTOK, DIM], F32)
        pay_d = dram("payload", [DUMMY_ROW + P, PAYW], F32)

        arena = ctx.enter_context(nc.sbuf_tensor("arena", [P, NE * WCOLS], F32))
        late = EARLY * WCOLS
        v_all = arena[:, late:late + NT * DIM].rearrange("p (t n) -> p t n", t=NT)
        spare = late + NT * DIM
        cst = ctx.enter_context(nc.sbuf_tensor("cst", [P, C_END], F32))
        ident = cst[:, C_ID:C_ID + P]
        identb = ctx.enter_context(nc.sbuf_tensor("eps_ones", [P, 2], F32))
        eps = identb[:, 0:1]
        slot_tab = ctx.enter_context(nc.sbuf_tensor("slot_tab", [1, 2, NSLOT], I32))
        s_cst = sem("consts_loaded")
        s_w = sem("expert_loaded")
        started = sem("started")
        gate = sem("passed")

        phase_project(nc, x, w_qkv, b_qkv, consts, rope, parts_d, w_exp, arena, v_all, cst, ident, eps, s_cst, s_w, started, gate)
        phase_attention(nc, w_exp, s_w, parts_d, att_d, v_all, arena, spare, cst, ident, gate)
        phase_route(nc, x, w_proj, b_proj, cent, att_d, pay_d, w_exp, arena, cst, ident, eps, slot_tab, s_w, gate)
        phase_ffn(nc, cols, b2, pay_d, arena, ident, slot_tab, s_w, out, gate)


def phase_project(nc, x, w_qkv, b_qkv, consts, rope, parts_d, w_exp, arena, v_all, cst, ident, eps, s_cst, s_w, started, gate):
    with ExitStack() as ctx:
        def sb(name, shape, dt=F32):
            return ctx.enter_context(nc.sbuf_tensor("A_" + name, shape, dt))

        def ps(name, shape, dt=F32):
            return ctx.enter_context(nc.psum_tensor("A_" + name, shape, dt))

        def sem(name):
            return ctx.enter_context(nc.semaphore("A_" + name))

        R = 4
        wq = sb("wq", [P, DC, 3 * DIM])
        bq = sb("bq", [P, 3 * DIM])
        rp = sb("rope_tab", [P, KB, 2 * HD])
        xt = sb("xt", [P, R, DIM])
        z = sb("z", [P, R, DIM])
        zt = sb("zt", [P, R, DC, P])
        qk = sb("qk", [P, R, 2 * DIM])
        t2 = sb("t2", [P, R, 2 * DIM])
        rot = sb("rot", [P, R, 2 * DIM])
        res = sb("res", [P, R, 2 * DIM])
        pt = sb("pt", [P, R, 4, NSPLIT, P], BF16)
        st = sb("st", [P, R, 6])
        mv = sb("mv", [P, R, 2])
        sd = sb("sd", [P, R, 2])
        ps_z = [ps(f"ps_z{i}", [P, DC * P]) for i in range(2)]
        ps_qk = [ps(f"ps_qk{i}", [P, 2 * DIM]) for i in range(2)]
        ps_v = [ps(f"ps_v{i}", [P, DIM]) for i in range(2)]
        ps_r = [ps(f"ps_r{i}", [P, 4 * P]) for i in range(2)]

        s_x = [sem(f"x_loaded{i}") for i in range(R)]
        s_wl = sem("weights_loaded")
        s_var = sem("variance")
        s_sd = sem("sqrt")
        s_rs = sem("dve_chain")
        s_z = sem("z_ready")
        s_tz = sem("z_transposed")
        s_zt = sem("zt_ready")
        s_mm = sem("projected")
        s_qk = sem("qk_biased")
        s_v = sem("v_biased")
        s_t1 = sem("cos_product")
        s_t2 = sem("sin_product")
        s_rot = sem("rotated")
        s_tr = sem("rotated_transposed")
        s_p1 = sem("part1")
        s_r1 = sem("rest1")
        s_p2 = sem("part2")
        s_p3 = sem("part3")
        s_st = [sem(f"parts_stored{i}") for i in range(R)]

        def steps(eng, emit):
            run_steps(eng, emit, -1, 8, 28, NT + 3, R)

        with nc.Block() as block:
            @block.sync
            def _(sp):
                sp.dma_start(cst[:, :], consts).then_inc(s_cst, 16)
                sp.dma_start(wq[:, :, :], w_qkv.rearrange("(c p) n -> p c n", p=P)).then_inc(s_wl, 16)
                sp.dma_start(bq[:, :], b_qkv.partition_broadcast(P)).then_inc(s_wl, 16)
                sp.dma_start(rp[:, :, :], rope.rearrange("(t p) n -> p t n", p=P)).then_inc(s_wl, 16)

                def load(T):
                    if T.within(NT):
                        wait(sp, s_z, T, 1, 1 - R, alone=gate)
                        sp.dma_start(xt[:, T.ring(R), :], x[bass.ds(T.value() * P, P), :]).then_inc(s_x[T.ring(R)], 16)

                for k in range(2):
                    load(Step(k))

                def emit(n):
                    load(n + 3)
                    T = n + -3
                    if T.within(NT):
                        wait(sp, s_p3, T, 1, 1, alone=gate)
                        for c in range(4):
                            kind, rows = c // 2, slice((c % 2) * P, (c % 2) * P + P)
                            sp.dma_start(
                                parts_d[kind, :, rows, bass.ds(T.value() * P, P)].rearrange("j p n -> p j n"),
                                pt[:, T.ring(R), c, :, :]).then_inc(s_st[T.ring(R)], 16)

                steps(sp, emit)
                for i in range(R):
                    sp.wait_ge(s_st[i], 64 * (NT // R))

            @block.scalar
            def _(act):
                act.wait_ge(started, 1)

                def emit(n):
                    T = n + 1
                    if T.within(NT):
                        r = T.ring(R)
                        wait(act, s_var, T, 1, 1)
                        act.activation(sd[:, r, 0:1], mv[:, r, 1:2], ACT.Sqrt, bias=eps).then_inc(s_sd, 1)
                    T = n + -3
                    if T.within(NT):
                        r = T.ring(R)
                        wait(act, s_tr, T, 1, 1)
                        if T.reg is not None or T.const >= R:
                            wait_dma(act, s_st, T + -R, 4)
                        act.activation(pt[:, r, :, 0, :], ps_r[r % 2][:, :].rearrange("p (c n) -> p c n", c=4),
                                       ACT.Copy).then_inc(s_p1, 1)
                        wait(act, s_r1, T, 1, 1)
                        act.activation(pt[:, r, :, 1, :], res[:, r, :].rearrange("p (c n) -> p c n", c=4),
                                       ACT.Copy).then_inc(s_p2, 1)
                    T = n + 1
                    if T.within(NT):
                        r = T.ring(R)
                        wait(act, s_tz, T, 1, 1)
                        wait(act, s_mm, T, 1, 1 - R)
                        act.activation(zt[:, r, :, :].rearrange("p c n -> p (c n)"), ps_z[r % 2][:, :], ACT.Copy).then_inc(s_zt, 1)

                steps(act, emit)

            @block.vector
            def _(dve):
                dve.memset(eps, EPS).then_inc(started, 1)
                dve.wait_ge(s_wl, 48)
                dve.wait_ge(s_cst, 16)

                def emit(n):
                    T = n + 1
                    if T.within(NT):
                        r = T.ring(R)
                        wait_dma(dve, s_x, T)
                        dve.bn_stats(st[:, r, :], xt[:, r, :]).then_inc(s_rs, 1)
                        wait(dve, s_rs, T, 2, 1, alone=gate)
                        dve.bn_aggr(mv[:, r, :], st[:, r, :]).then_inc(s_var, 1)
                    T = n + -3
                    if T.within(NT):
                        r = T.ring(R)
                        wait(dve, s_p1, T, 1, 1)
                        dve.tensor_tensor(res[:, r, :].rearrange("p (c n) -> p c n", c=4),
                                          ps_r[r % 2][:, :].rearrange("p (c n) -> p c n", c=4),
                                          pt[:, r, :, 0, :], ALU.subtract).then_inc(s_r1, 1)
                    T = n + 1
                    if T.within(NT):
                        r = T.ring(R)
                        wait(dve, s_sd, T, 1, 1)
                        dve.reciprocal(sd[:, r, 1:2], sd[:, r, 0:1]).then_inc(s_rs, 1)
                        wait(dve, s_rs, T, 2, 2)
                        wait(dve, s_tz, T, 1, 1 - R)
                        dve.tensor_scalar(z[:, r, :], xt[:, r, :], mv[:, r, 0:1], sd[:, r, 1:2],
                                          ALU.subtract, ALU.mult).then_inc(s_z, 1)
                    T = n + -1
                    if T.within(NT):
                        r = T.ring(R)
                        wait(dve, s_mm, T, 1, 1)
                        wait(dve, s_rot, T, 1, 1 - R)
                        dve.tensor_tensor(qk[:, r, :], ps_qk[r % 2][:, :], bq[:, 0:2 * DIM], ALU.add).then_inc(s_qk, 1)
                        dve.tensor_tensor(v_all[:, bass.ds(T.value(), 1), :].rearrange("p a n -> p (a n)"),
                                          ps_v[r % 2][:, :], bq[:, 2 * DIM:3 * DIM], ALU.add).then_inc(s_v, 1)
                        cos = rp[:, bass.ds(T.value() % KB, 1), 0:HD].to_broadcast([P, 2 * HEADS, HD])
                        wait(dve, s_qk, T, 1, 1)
                        wait(dve, s_tr, T, 1, 1 - R)
                        dve.tensor_tensor(rot[:, r, :].rearrange("p (h d) -> p h d", d=HD),
                                          qk[:, r, :].rearrange("p (h d) -> p h d", d=HD), cos, ALU.mult).then_inc(s_t1, 1)
                        wait(dve, s_t1, T, 1, 1)
                        wait(dve, s_t2, T, 2, 2)
                        dve.tensor_tensor(rot[:, r, :], rot[:, r, :], t2[:, r, :], ALU.add).then_inc(s_rot, 1)

                steps(dve, emit)

            @block.gpsimd
            def _(pool):
                def emit(n):
                    T = n + -1
                    if T.within(NT):
                        r = T.ring(R)
                        wait(pool, s_qk, T, 1, 1, alone=gate)
                        wait(pool, s_rot, T, 1, 1 - R, alone=gate)
                        src = qk[:, r, :].rearrange("p (h s d) -> p h s d", s=2, d=HD // 2)
                        dst = t2[:, r, :].rearrange("p (h s d) -> p h s d", s=2, d=HD // 2)
                        for s in range(2):
                            sin = rp[:, bass.ds(T.value() % KB, 1), HD + s * HD // 2:HD + (s + 1) * HD // 2]
                            pool.tensor_tensor(dst[:, :, s, :], src[:, :, 1 - s, :],
                                               sin.to_broadcast([P, 2 * HEADS, HD // 2]), ALU.mult).then_inc(s_t2, 1)
                    T = n + -3
                    if T.within(NT):
                        r = T.ring(R)
                        wait(pool, s_p2, T, 1, 1, alone=gate)
                        pool.tensor_tensor(pt[:, r, :, 2, :], res[:, r, :].rearrange("p (c n) -> p c n", c=4),
                                           pt[:, r, :, 1, :], ALU.subtract).then_inc(s_p3, 1)

                steps(pool, emit)

            @block.tensor
            def _(pe):
                pe.wait_ge(s_cst, 16)
                pe.wait_ge(s_wl, 48)

                def emit(n):
                    T = n
                    if T.within(NT):
                        r = T.ring(R)
                        wait(pe, s_zt, T, 1, 1)
                        wait(pe, s_qk, T, 1, -1)
                        for c in range(DC):
                            pe.matmul(ps_qk[r % 2][:, :], zt[:, r, c, :], wq[:, c, 0:2 * DIM], start=(c == 0), stop=(c == DC - 1))
                        wait(pe, s_v, T, 1, -1)
                        for c in range(DC):
                            mm = pe.matmul(ps_v[r % 2][:, :], zt[:, r, c, :], wq[:, c, 2 * DIM:3 * DIM], start=(c == 0), stop=(c == DC - 1))
                        mm.then_inc(s_mm, 1)
                    T = n + 1
                    if T.within(NT):
                        r = T.ring(R)
                        wait(pe, s_z, T, 1, 1)
                        wait(pe, s_zt, T, 1, -1)
                        for c in range(DC):
                            mm = pe.transpose(ps_z[r % 2][:, c * P:(c + 1) * P], z[:, r, c * P:(c + 1) * P], ident)
                        mm.then_inc(s_tz, 1)
                    T = n + -2
                    if T.within(NT):
                        r = T.ring(R)
                        wait(pe, s_rot, T, 1, 1)
                        wait(pe, s_r1, T, 1, -1)
                        for c in range(4):
                            mm = pe.transpose(ps_r[r % 2][:, c * P:(c + 1) * P], rot[:, r, c * P:(c + 1) * P], ident)
                        mm.then_inc(s_tr, 1)

                steps(pe, emit)


def phase_attention(nc, w_exp, s_w, parts_d, att_d, v_all, arena, spare, cst, ident, gate):
    with ExitStack() as ctx:
        def sb(name, shape, dt=F32):
            return ctx.enter_context(nc.sbuf_tensor("B_" + name, shape, dt))

        def ps(name, shape, dt=F32):
            return ctx.enter_context(nc.psum_tensor("B_" + name, shape, dt))

        def sem(name):
            return ctx.enter_context(nc.semaphore("B_" + name))

        R = 3
        SUB = KB + KB // 2
        LATE = 4
        NU = QH * SUB
        scale = float(HD) ** -0.5

        qs = sb("q_stack", [SROWS + MROWS, R, QH, SEQ], BF16)
        ks = sb("k_stack", [SROWS + MROWS, R, QH, SEQ], BF16)
        vq = sb("v_quad", [P, R, KB, QH, 32])
        pr = arena[:, spare:spare + 2 * QH * QW].rearrange("p (r h n) -> p r h n", r=2, h=QH)
        dump = sb("max_dump", [P, 2, QW], BF16)
        mx = sb("mx", [P, 2, QH * KB])
        mc = sb("mc", [P, QH * KB])
        nm = sb("nm", [QH * KB, MROWS, P], BF16)
        nr = sb("nr", [QH * KB, P])
        oacc = sb("oacc", [P, 2, QW])
        rec = sb("rec", [P, 2, QH * QH])
        ost = sb("ost", [P, 2, QH, QH * HD])
        ps_s = [ps(f"ps_s{i}", [P, 2, QW]) for i in range(2)]
        ps_m = [ps(f"ps_m{i}", [P, QW]) for i in range(2)]
        ps_o = ps("ps_o", [P, QW])
        ps_t = ps("ps_t", [P, 4, P])

        s_stk = [sem(f"stack_loaded{i}") for i in range(R)]
        s_ones = sem("preset")
        s_vone = sem("v_preset")
        s_vq = sem("v_quad")
        s_mm = sem("max_scores")
        s_mr = sem("max_reduced")
        s_mc = sem("max_combined")
        s_mt = sem("max_transposed")
        s_n1 = sem("max_part1")
        s_nr = sem("max_rest")
        s_n2 = sem("max_part2")
        s_n3 = sem("max_part3")
        s_row = sem("max_rows_loaded")
        s_s = sem("scores")
        s_e = sem("exp")
        s_k = sem("masked")
        s_pv = sem("pv")
        s_oe = sem("out_evacuated")
        s_ot = sem("out_transposed")
        s_rc = sem("reciprocal")
        s_on = sem("out_normed")
        s_os = [sem(f"out_stored{i}") for i in range(2)]

        subs = [(c, kb, max(0, kb - 4 * c) * P) for c in range(2) for kb in range(4 * c + 4)]
        diag = [i for i, (c, kb, _) in enumerate(subs) if kb >= 4 * c]
        ends = [max(i for i, s in enumerate(subs) if s[0] == c) for c in range(2)]
        units = [(h, t, a) for h in range(QH) for t in range(KB) for a in range(t // 4 + 1)]
        assert len(units) == NU and len(subs) == SUB
        norm_at = {1: LATE + 2, 0: LATE + 6}

        def sub_at(i, k):
            return (i + -1, k + SUB - LATE) if k < LATE else (i, k - LATE)

        def steps(eng, emit):
            run_steps(eng, emit, -1, 2, 14, NQ + 1, R)

        with nc.Block() as block:
            @block.sync
            def _(sp):
                def load(Q):
                    r = Q.ring(R)
                    wait(sp, s_s, Q, 2 * SUB, -2 * SUB * (R - 1), alone=gate)
                    q = Q.value()
                    rows, toks = bass.ds((q % QB) * (QH * HD), QH * HD), bass.ds((q // QB) * SEQ, SEQ)

                    def put(stack, at, width, kind, part):
                        sp.dma_start(stack[at:at + HD * width:width, r, :, :],
                                     parts_d[kind, part, rows, toks].rearrange("(h d) n -> d h n", d=HD)).then_inc(s_stk[r], 16)

                    for at, width, qp in ((0, 3, 0), (3 * HD, 2, 1), (5 * HD, 1, 2)):
                        for j in range(width):
                            put(qs, at + j, width, 0, qp)
                            put(ks, at + j, width, 1, j)

                load(Step(0))

                def emit(n):
                    if n.reg is None and n.const == -1:
                        load(Step(1))
                    if n.within(NQ):
                        wait(sp, s_n3, n, 1, 1, alone=gate)
                        for j in range(MROWS):
                            sp.dma_start(qs[SROWS + j:SROWS + j + 1, n.ring(R), :, :], nm[:, j, :]).then_inc(s_row, 16)
                    Q = n + 2
                    if (Q.within(NQ)) and not (Q.reg is None and Q.const < 2):
                        load(Q)
                    for Q, c in ((n + -1, 1), (n, 0)):
                        if Q.within(NQ):
                            wait(sp, s_on, Q, 2, c + 1, alone=gate)
                            q = Q.value()
                            sp.dma_start(
                                att_d[bass.ds((q // QB) * SEQ + c * QW, QW), bass.ds((q % QB) * (QH * HD), QH * HD)]
                                .rearrange("(t p) n -> p t n", p=P), ost[:, c, :, :]).then_inc(s_os[c], 16)

                steps(sp, emit)
                for c in range(2):
                    sp.wait_ge(s_os[c], 16 * NQ)

            @block.gpsimd
            def _(pool):
                pool.memset(vq[:, :, :, :, :], 1.0).then_inc(s_vone, 1)
                pool.wait_ge(s_vone, 1)
                for e in range(EARLY):
                    pool.dma_start(arena[:, e * WCOLS:(e + 1) * WCOLS], w_exp[e]).then_inc(s_w, 16)


                def emit(i):
                    Q = i + 1
                    if Q.within(NQ):
                        wait(pool, s_pv, Q, SUB, -SUB * (R - 1), alone=gate)
                        q = Q.value()
                        pool.tensor_copy(
                            vq[:, Q.ring(R), :, :, 0:HD],
                            v_all[:, bass.ds((q // QB) * KB, KB), bass.ds((q % QB) * (QH * HD), QH * HD)]
                            .rearrange("p t (h d) -> p t h d", h=QH)).then_inc(s_vq, 1)
                    for k in range(SUB):
                        if k == 1 and i.within(NQ):
                            wait(pool, s_nr, i, 1, 1, alone=gate)
                            pool.tensor_copy(nm[:, 1, :], nr[:, :]).then_inc(s_n2, 1)
                            wait(pool, s_n2, i, 1, 1, alone=gate)
                            pool.tensor_tensor(nm[:, 2, :], nr[:, :], nm[:, 1, :], ALU.subtract).then_inc(s_n3, 1)
                        Q, s = sub_at(i, k)
                        if Q.within(NQ) and s in diag:
                            wait(pool, s_e, Q, 2 * SUB, 2 * s + 2, alone=gate)
                            tri = pr[:, s % 2, :, 0:P]
                            pool.affine_select(out=tri, in_=tri, compare_op=ALU.is_ge, fill=0.0, base=0,
                                               pattern=[[0, QH], [1, P]], channel_multiplier=-1).then_inc(s_k, 1)

                steps(pool, emit)
                pool.wait_ge(s_w, 16 * EARLY)

            @block.scalar
            def _(act):
                def emit(i):
                    for k in range(SUB):
                        Q, s = sub_at(i, k)
                        if not Q.within(NQ):
                            continue
                        c, kb, off = subs[s]
                        wait(act, s_pv, Q, SUB, s - 1)
                        for p in range(2):
                            wait(act, s_s, Q, 2 * SUB, 2 * s + p + 1)
                            act.activation(pr[:, s % 2, 2 * p:2 * p + 2, 0:QW - off], ps_s[p][:, :, 0:QW - off],
                                           ACT.Exp, scale=scale).then_inc(s_e, 1)
                        if s > 0 and s - 1 in ends or s == 0:
                            QE, ce = (Q, 0) if s > 0 else (Q + -1, 1)
                            if QE.within(NQ):
                                evac(QE, ce)
                    if i.reg is None and i.const == NQ:
                        evac(Step(NQ - 1), 1)

                def evac(Q, c):
                    wait(act, s_pv, Q, SUB, ends[c] + 1)
                    wait(act, s_ot, Q, 2, c - 1)
                    act.activation(oacc[:, c, :], ps_o[:, :], ACT.Copy).then_inc(s_oe, 1)

                steps(act, emit)

            @block.vector
            def _(dve):
                dve.memset(mx[:, :, :], NEG).then_inc(s_ones, 1)
                dve.memset(ks[SROWS:SROWS + MROWS, :, :, :], 1.0).then_inc(s_ones, 1)
                dve.wait_ge(s_ones, 2)

                def norm(Q, c):
                    wait(dve, s_ot, Q, 2, c + 1)
                    view = ps_t[:, :, :].rearrange("p t (h d) -> p (t h) d", h=QH)
                    dve.reciprocal(rec[:, c, :], view[:, :, HD]).then_inc(s_rc, 1)
                    wait(dve, s_rc, Q, 2, c + 1)
                    if Q.reg is not None or Q.const >= 1:
                        if Q.reg is None:
                            dve.wait_ge(s_os[c], 16 * Q.const)
                        else:
                            dve.wait_ge(s_os[c], Q.value() * 16)
                    dve.tensor_tensor(ost[:, c, :, :].rearrange("p t (h d) -> p (t h) d", h=QH), view[:, :, 0:HD],
                                      rec[:, c, :].unsqueeze(2).to_broadcast([P, QH * QH, HD]), ALU.mult).then_inc(s_on, 1)

                def emit(i):
                    M = i + 1
                    for k in range(SUB):
                        if k == 1 and i.within(NQ):
                            wait(dve, s_mt, i, 1, 1)
                            wait(dve, s_row, i, 16 * MROWS, 0)
                            dve.tensor_scalar(nm[:, 0, :], ps_t[0:QH * KB, 0, :], -1.0, None, ALU.mult).then_inc(s_n1, 1)
                            wait(dve, s_n1, i, 1, 1)
                            dve.scalar_tensor_tensor(out=nr[:, :], in0=ps_t[0:QH * KB, 0, :], scalar=-1.0, in1=nm[:, 0, :],
                                                     op0=ALU.mult, op1=ALU.subtract).then_inc(s_nr, 1)
                        for u in range(4 * k, 4 * k + 4):
                            if M.within(NQ):
                                h, t, a = units[u]
                                n = min(QW, (t + 1) * P - a * QW)
                                wait(dve, s_mm, M, NU, u + 1, alone=gate)
                                if u == 0:
                                    wait(dve, s_mc, M, 1, 0, alone=gate)
                                col = mx[:, a, h * KB + t:h * KB + t + 1]
                                if a == t // 4:
                                    dve.tensor_tensor_reduce(dump[:, u % 2, 0:n], ps_m[u % 2][:, 0:n],
                                                             cst[:, C_MASK + QW - n:C_MASK + QW], 1.0, NEG,
                                                             ALU.add, ALU.max, col).then_inc(s_mr, 1)
                                else:
                                    dve.tensor_reduce(col, ps_m[u % 2][:, 0:n], AX.X, ALU.max).then_inc(s_mr, 1)
                        for Q, c in ((i + -1, 1), (i, 0)):
                            if Q.within(NQ) and k == norm_at[c]:
                                norm(Q, c)
                    if M.within(NQ):
                        wait(dve, s_mr, M, NU, NU)
                        wait(dve, s_mt, M, 1, 0)
                        dve.tensor_tensor(mc[:, :], mx[:, 0, :], mx[:, 1, :], ALU.max).then_inc(s_mc, 1)

                steps(dve, emit)

            @block.tensor
            def _(pe):
                pe.wait_ge(s_ones, 2)

                def max_unit(M, u):
                    if not M.within(NQ):
                        return
                    h, t, a = units[u]
                    r = M.ring(R)
                    n = min(QW, (t + 1) * P - a * QW)
                    if u == 0:
                        wait_dma(pe, s_stk, M, 12)
                    wait(pe, s_mr, M, NU, u - 1)
                    pe.matmul(ps_m[u % 2][:, 0:n], qs[0:SROWS, r, h, t * P:(t + 1) * P],
                              ks[0:SROWS, r, h, a * QW:a * QW + n], start=True, stop=True).then_inc(s_mm, 1)

                def scores(Q, s, p):
                    c, kb, off = subs[s]
                    r = Q.ring(R)
                    if s == 0 and p == 0:
                        wait(pe, s_row, Q, 16 * MROWS, 16 * MROWS)
                    wait(pe, s_e, Q, 2 * SUB, 2 * s + p - 1)
                    for j in range(2):
                        h = 2 * p + j
                        mm = pe.matmul(ps_s[p][:, j, 0:QW - off], ks[:, r, h, kb * P:(kb + 1) * P],
                                       qs[:, r, h, c * QW + off:(c + 1) * QW], start=True, stop=True)
                    mm.then_inc(s_s, 1)

                def pv(Q, s):
                    c, kb, off = subs[s]
                    r = Q.ring(R)
                    wait(pe, s_e, Q, 2 * SUB, 2 * s + 2)
                    if s in diag:
                        wait(pe, s_k, Q, len(diag), diag.index(s) + 1)
                    if s == 0:
                        wait(pe, s_vq, Q, 1, 1)
                    if kb == 0:
                        wait(pe, s_oe, Q, 2, c)
                    for h in range(QH):
                        mm = pe.matmul(ps_o[32 * h:32 * h + 32, off:QW], vq[:, r, kb, h, :], pr[:, s % 2, h, 0:QW - off],
                                       start=(kb == 0), stop=(kb == 4 * c + 3), tile_position=(0, 32 * h))
                    mm.then_inc(s_pv, 1)

                def out_transpose(Q, c):
                    wait(pe, s_oe, Q, 2, c + 1)
                    if c == 1:
                        wait(pe, s_nr, Q + 1, 1, 1) if (Q + 1).within(NQ) else None
                    wait(pe, s_on, Q, 2, c)
                    for t in range(4):
                        mm = pe.transpose(ps_t[:, t, :], oacc[:, c, t * P:(t + 1) * P], ident)
                    mm.then_inc(s_ot, 1)

                def emit(i):
                    M = i + 1
                    for k in range(SUB):
                        if k == 1 and i.within(NQ):
                            wait(pe, s_mc, i, 1, 1)
                            wait(pe, s_on, i, 2, -1)
                            pe.transpose(ps_t[0:QH * KB, 0, :], mc[:, :], ident).then_inc(s_mt, 1)
                        Q, s = sub_at(i, k)
                        before = (Q, s - 1) if s > 0 else (Q + -1, SUB - 1)
                        for p in range(2):
                            if Q.within(NQ):
                                scores(Q, s, p)
                            max_unit(M, 4 * k + p)
                        if before[0].within(NQ):
                            pv(*before)
                        for u in (2, 3):
                            max_unit(M, 4 * k + u)
                        for Q, c in ((i + -1, 1), (i, 0)):
                            if Q.within(NQ) and k == norm_at[c]:
                                out_transpose(Q, c)

                steps(pe, emit)




def phase_route(nc, x, w_proj, b_proj, cent, att_d, pay_d, w_exp, arena, cst, ident, eps, slot_tab, s_w, gate):
    with ExitStack() as ctx:
        def sb(name, shape, dt=F32):
            return ctx.enter_context(nc.sbuf_tensor("C_" + name, shape, dt))

        def ps(name, shape, dt=F32):
            return ctx.enter_context(nc.psum_tensor("C_" + name, shape, dt))

        def sem(name):
            return ctx.enter_context(nc.semaphore("C_" + name))

        R = 4
        wp = sb("wp", [P, DC, DIM])
        bp = sb("bp", [P, DIM])
        ct = sb("centroids", [P, DC, NE])
        ot = sb("ot", [P, R, DIM])
        xt = sb("xt", [P, R, DIM])
        oT = sb("oT", [P, R, DC, P])
        zT = sb("zT", [P, R, DC, P])
        x2 = sb("x2", [P, R, DIM])
        z = sb("z", [P, R, DIM])
        pay = sb("pay", [P, R, PAYW])
        st = sb("st", [P, R, 2, 6])
        mv = sb("mv", [P, R, 2, 2])
        sd = sb("sd", [P, R, 2, 2])
        top = sb("top", [P, R, 8])
        ge = sb("ge", [P, R, NE])
        pick = sb("pick", [P, R, NE])
        pm = sb("pm", [P, R, 1])
        hot = sb("hot", [P, R, NE], BF16)
        hotf = sb("hotf", [P, R, NE])
        seen = sb("seen", [P, NE])
        rank = sb("rank", [P, R, NE])
        posf = sb("posf", [P, R, 2])
        posi = sb("posi", [P, R, 1], I32)
        lt = sb("lt", [P, 2, P], BF16)
        padrow = sb("padrow", [P, PAYW])
        padidx = sb("padidx", [P, NE], I32)
        cnt = sb("cnt", [P, NE])
        more = sb("more", [P, NE, NT])
        ns = sb("ns", [P, 4, NE])
        tab = sb("tab", [1, NSLOT, NE])
        tab2 = sb("tab2", [1, NSLOT, NE])
        es = sb("es", [1, 4, NSLOT])
        ps_o = [ps(f"ps_o{i}", [P, DC * P]) for i in range(2)]
        ps_p = [ps(f"ps_p{i}", [P, DIM]) for i in range(2)]
        ps_z = ps("ps_z", [P, DC * P])
        ps_a = [ps(f"ps_a{i}", [P, NE]) for i in range(2)]
        ps_k = ps("ps_k", [P, 2, NE])

        s_in = [sem(f"in_loaded{i}") for i in range(R)]
        s_wl = sem("weights_loaded")
        s_pre = sem("preset")
        s_pad0 = sem("pad_zeroed")
        s_xb = sem("x_biased")
        s_to = sem("o_transposed")
        s_ot = sem("oT_ready")
        s_pj = sem("projected")
        s_x2 = sem("x2")
        s_c = sem("dve_chain")
        s_v1 = sem("var1")
        s_d1 = sem("sqrt1")
        s_z = sem("z_ready")
        s_v2 = sem("var2")
        s_d2 = sem("sqrt2")
        s_zz = sem("zz_ready")
        s_tz = sem("z_transposed")
        s_zt = sem("zT_ready")
        s_af = sem("affinity")
        s_hot = sem("one_hot")
        s_ge, s_rs, s_end = sem("one_hot_chain"), sem("position_chain"), sem("table_chain")
        s_rk = sem("rank_products")
        s_sn = sem("seen")
        s_ps = sem("position")
        s_b = sem("base_ready")
        s_sc = [sem(f"scattered{i}") for i in range(R)]
        s_tb = sem("table")
        s_late = sem("late_expert_loaded")
        s_pad = sem("pads_written")
        s_dum = sem("dummy_rows_written")

        late_at = [0, 5, 26]
        assert len(late_at) == NE - EARLY

        def steps(eng, emit):
            run_steps(eng, emit, -2, 6, 26, NT + 2, R)

        with nc.Block() as block:
            @block.sync
            def _(sp):
                sp.dma_start(wp[:, :, :], w_proj.rearrange("(c p) n -> p c n", p=P)).then_inc(s_wl, 16)
                sp.dma_start(bp[:, :], b_proj.partition_broadcast(P)).then_inc(s_wl, 16)
                sp.dma_start(ct[:, :, :], cent.rearrange("(c p) n -> p c n", p=P)).then_inc(s_wl, 16)

                def load(T):
                    if T.within(NT):
                        r = T.ring(R)
                        wait(sp, s_x2, T, 1, 1 - R, alone=gate)
                        sp.dma_start(ot[:, r, :], att_d[bass.ds(T.value() * P, P), :]).then_inc(s_in[r], 16)
                        sp.dma_start(xt[:, r, :], x[bass.ds(T.value() * P, P), :]).then_inc(s_in[r], 16)

                load(Step(0))

                def emit(n):
                    load(n + 3)
                    if n.reg is None and n.const in late_at:
                        e = EARLY + late_at.index(n.const)
                        if e > EARLY:
                            sp.wait_ge(s_late, 16 * (e - EARLY))
                        sp.dma_start(arena[:, e * WCOLS:(e + 1) * WCOLS], w_exp[e]).then_inc(s_late, 16)

                steps(sp, emit)
                sp.wait_ge(s_late, 16 * (NE - EARLY))
                sp.wait_ge(s_pre, 4)
                sp.dma_start(pay_d[DUMMY_ROW:DUMMY_ROW + P, :], padrow[:, :]).then_inc(s_dum, 16)
                sp.wait_ge(s_dum, 16)

            @block.gpsimd
            def _(pool):
                pool.memset(padrow[:, :], 0.0).then_inc(s_pad0, 1)
                pool.wait_ge(s_wl, 48)

                def emit(n):
                    T = n
                    if T.within(NT):
                        r = T.ring(R)
                        wait_dma(pool, s_in, T, 2, alone=gate)
                        pool.tensor_tensor(xt[:, r, :], xt[:, r, :], bp[:, :], ALU.add).then_inc(s_xb, 1)
                    T = n
                    if T.within(NT):
                        r = T.ring(R)
                        wait(pool, s_z, T, 1, 1, alone=gate)
                        if T.reg is not None or T.const >= R:
                            wait_dma(pool, s_sc, T + -R, alone=gate)
                        pool.tensor_tensor(pay[:, r, DIM:2 * DIM], x2[:, r, :], z[:, r, :], ALU.add).then_inc(s_b, 1)
                        pool.tensor_copy(pay[:, r, 2 * DIM + 1:2 * DIM + 2].bitcast(I32),
                                         cst[:, bass.ds(T.value() + C_ID32, 1)].bitcast(I32)).then_inc(s_b, 1)
                    T = n + -2
                    if T.within(NT):
                        r = T.ring(R)
                        wait(pool, s_ps, T, 1, 1, alone=gate)
                        wait(pool, s_zz, T, 1, 1, alone=gate)
                        wait(pool, s_b, T, 2, 2, alone=gate)
                        pool.indirect_dma_start(pay_d[:, :], bass.IndirectOffsetOnAxis(ap=posi[:, r, :].bitcast(U32), axis=0),
                                                pay[:, r, :], None).then_inc(s_sc[r], 16)

                steps(pool, emit)
                pool.wait_ge(s_tb, 2)
                for e in range(NE):
                    pool.indirect_dma_start(pay_d[:, :], bass.IndirectOffsetOnAxis(ap=padidx[:, e:e + 1].bitcast(U32), axis=0),
                                            padrow[:, :], None).then_inc(s_pad, 16)
                pool.wait_ge(s_pad, 16 * NE)
                for i in range(R):
                    pool.wait_ge(s_sc[i], 16 * (NT // R))

            @block.scalar
            def _(act):
                def emit(n):
                    T = n + -1
                    if T.within(NT):
                        r = T.ring(R)
                        wait(act, s_tz, T, 1, 1)
                        wait(act, s_af, T, 1, 1 - R)
                        act.activation(zT[:, r, :, :].rearrange("p c n -> p (c n)"), ps_z[:, :], ACT.Copy).then_inc(s_zt, 1)
                    T = n + 2
                    if T.within(NT):
                        r = T.ring(R)
                        wait(act, s_to, T, 1, 1)
                        wait(act, s_pj, T, 1, 1 - R)
                        act.activation(oT[:, r, :, :].rearrange("p c n -> p (c n)"), ps_o[r % 2][:, :], ACT.Copy).then_inc(s_ot, 1)
                    T = n
                    if T.within(NT):
                        r = T.ring(R)
                        wait(act, s_v1, T, 1, 1)
                        act.activation(sd[:, r, 0, 0:1], mv[:, r, 0, 1:2], ACT.Sqrt, bias=eps).then_inc(s_d1, 1)
                        wait(act, s_v2, T, 1, 1)
                        act.activation(sd[:, r, 1, 0:1], mv[:, r, 1, 1:2], ACT.Sqrt, bias=eps).then_inc(s_d2, 1)

                steps(act, emit)

            @block.vector
            def _(dve):
                dve.tensor_copy(lt[:, 0, :], cst[:, C_LT:C_LT + P]).then_inc(s_pre, 1)
                dve.memset(lt[:, 1, :], 1.0).then_inc(s_pre, 1)
                dve.tensor_scalar(seen[:, :], cst[:, C_IOTA:C_IOTA + NE], float(REGION), None, ALU.mult).then_inc(s_pre, 1)
                dve.wait_ge(s_pad0, 1)
                dve.tensor_copy(padrow[:, 2 * DIM + 1:2 * DIM + 2].bitcast(I32),
                                cst[:, C_IOTAP + 0:C_IOTAP + 1].bitcast(I32)).then_inc(s_pre, 1)
                dve.wait_ge(s_wl, 48)
                CH = 4

                def emit(n):
                    T = n
                    if T.within(NT):
                        r = T.ring(R)
                        wait(dve, s_pj, T, 1, 1)
                        wait(dve, s_xb, T, 1, 1)
                        wait(dve, s_b, T, 2, -2 * R + 1)
                        dve.tensor_tensor(x2[:, r, :], ps_p[r % 2][:, :], xt[:, r, :], ALU.add).then_inc(s_x2, 1)
                        wait(dve, s_x2, T, 1, 1)
                        dve.bn_stats(st[:, r, 0, :], x2[:, r, :]).then_inc(s_c, 1)
                        wait(dve, s_c, T, CH, 1, alone=gate)
                        dve.bn_aggr(mv[:, r, 0, :], st[:, r, 0, :]).then_inc(s_v1, 1)
                    T = n + -2
                    if T.within(NT):
                        r = T.ring(R)
                        wait(dve, s_af, T, 1, 1)
                        dve.tensor_reduce(top[:, r, 0:1], ps_a[r % 2][:, :], AX.X, ALU.max).then_inc(s_ge, 1)
                        wait(dve, s_ge, T, 5, 1)
                        dve.tensor_scalar(ge[:, r, :], ps_a[r % 2][:, :], top[:, r, 0:1], None, ALU.is_ge).then_inc(s_ge, 1)
                        wait(dve, s_ge, T, 5, 2)
                        dve.tensor_tensor(pick[:, r, :], ge[:, r, :], cst[:, C_RIOTA:C_RIOTA + NE], ALU.mult).then_inc(s_ge, 1)
                        wait(dve, s_ge, T, 5, 3)
                        dve.tensor_reduce(pm[:, r, :], pick[:, r, :], AX.X, ALU.max).then_inc(s_ge, 1)
                        wait(dve, s_ge, T, 5, 4)
                        dve.tensor_scalar(hot[:, r, :], cst[:, C_RIOTA:C_RIOTA + NE], pm[:, r, :], None, ALU.is_equal).then_inc(s_hot, 1)
                        dve.tensor_scalar(hotf[:, r, :], cst[:, C_RIOTA:C_RIOTA + NE], pm[:, r, :], None, ALU.is_equal).then_inc(s_ge, 1)
                    T = n
                    if T.within(NT):
                        r = T.ring(R)
                        wait(dve, s_d1, T, 1, 1)
                        dve.reciprocal(sd[:, r, 0, 1:2], sd[:, r, 0, 0:1]).then_inc(s_c, 1)
                        wait(dve, s_c, T, CH, 2)
                        wait(dve, s_tz, T, 1, 1 - R)
                        dve.tensor_scalar(z[:, r, :], x2[:, r, :], mv[:, r, 0, 0:1], sd[:, r, 0, 1:2],
                                          ALU.subtract, ALU.mult).then_inc(s_z, 1)
                        wait(dve, s_z, T, 1, 1)
                        dve.bn_stats(st[:, r, 1, :], z[:, r, :]).then_inc(s_c, 1)
                        wait(dve, s_c, T, CH, 3, alone=gate)
                        dve.bn_aggr(mv[:, r, 1, :], st[:, r, 1, :]).then_inc(s_v2, 1)
                    T = n + -2
                    if T.within(NT):
                        r = T.ring(R)
                        wait(dve, s_rk, T, 1, 1)
                        wait(dve, s_sn, T, 1, 0)
                        dve.tensor_tensor(rank[:, r, :], ps_k[:, 0, :], seen[:, :], ALU.add).then_inc(s_rs, 1)
                        wait(dve, s_rs, T, 3, 1)
                        wait(dve, s_ge, T, 5, 5)
                        dve.tensor_tensor_reduce(ge[:, r, :], rank[:, r, :], hotf[:, r, :], 1.0, 0.0, ALU.mult, ALU.add,
                                                 posf[:, r, 0:1]).then_inc(s_rs, 1)
                        dve.tensor_tensor(seen[:, :], ps_k[:, 1, :], seen[:, :], ALU.add).then_inc(s_sn, 1)
                        wait(dve, s_rs, T, 3, 2)
                        if T.reg is not None or T.const >= R:
                            wait_dma(dve, s_sc, T + -R)
                        dve.tensor_copy(pay[:, r, 2 * DIM:2 * DIM + 1], top[:, r, 0:1]).then_inc(s_rs, 1)
                        dve.tensor_copy(posi[:, r, :], posf[:, r, 0:1]).then_inc(s_ps, 1)
                    T = n
                    if T.within(NT):
                        r = T.ring(R)
                        wait(dve, s_d2, T, 1, 1)
                        dve.reciprocal(sd[:, r, 1, 1:2], sd[:, r, 1, 0:1]).then_inc(s_c, 1)
                        wait(dve, s_c, T, CH, 4)
                        if T.reg is not None or T.const >= R:
                            wait_dma(dve, s_sc, T + -R)
                        dve.tensor_scalar(pay[:, r, 0:DIM], z[:, r, :], mv[:, r, 1, 0:1], sd[:, r, 1, 1:2],
                                          ALU.subtract, ALU.mult).then_inc(s_zz, 1)

                steps(dve, emit)

                link = [0]

                def chain(ins):
                    link[0] += 1
                    ins.then_inc(s_end, 1)
                    dve.wait_ge(s_end, link[0])

                dve.wait_ge(s_sn, NT)
                chain(dve.tensor_copy(posf[:, 0, 0:1], cst[:, C_IOTAP:C_IOTAP + 1].bitcast(I32)))
                chain(dve.tensor_scalar(posf[:, 0, 1:2], posf[:, 0, 0:1], -float(NTOK), None, ALU.add))
                chain(dve.tensor_scalar(rank[:, 0, :], seen[:, :], posf[:, 0, 1:2], None, ALU.add))
                dve.tensor_copy(padidx[:, :], rank[:, 0, :]).then_inc(s_tb, 1)
                chain(dve.scalar_tensor_tensor(out=cnt[:, :], in0=cst[:, C_IOTA:C_IOTA + NE], scalar=-float(REGION), in1=seen[:, :],
                                               op0=ALU.mult, op1=ALU.add))
                chain(dve.tensor_tensor(more[:, :, :], cnt[:, :].unsqueeze(2).to_broadcast([P, NE, NT]),
                                        cst[:, C_BLK:C_BLK + NT].unsqueeze(1).to_broadcast([P, NE, NT]), ALU.is_gt))
                chain(dve.tensor_reduce(ns[:, 0, :], more[:, :, :], AX.X, ALU.add))
                chain(dve.tensor_copy(ns[:, 1, :], ns[:, 0, :]))
                a, b = 1, 2
                for d in (1, 2, 4):
                    chain(dve.tensor_copy(ns[:, b, 0:d], ns[:, a, 0:d]))
                    chain(dve.tensor_tensor(ns[:, b, d:NE], ns[:, a, d:NE], ns[:, a, 0:NE - d], ALU.add))
                    a, b = b, a
                chain(dve.tensor_tensor(ns[:, 3, :], ns[:, a, :], ns[:, 0, :], ALU.subtract))
                chain(dve.tensor_scalar(ns[:, 3, :], ns[:, 3, :], -float(P), None, ALU.mult))
                chain(dve.scalar_tensor_tensor(out=ns[:, 3, :], in0=cst[:, C_IOTA:C_IOTA + NE], scalar=float(REGION),
                                               in1=ns[:, 3, :], op0=ALU.mult, op1=ALU.add))
                slots = cst[0:1, C_SLOT:C_SLOT + NSLOT]
                by_slot = slots.unsqueeze(2).to_broadcast([1, NSLOT, NE])
                chain(dve.tensor_tensor(tab[:, :, :], by_slot, ns[0:1, a, :].unsqueeze(1).to_broadcast([1, NSLOT, NE]), ALU.is_ge))
                chain(dve.tensor_reduce(es[:, 0, :], tab[:, :, :], AX.X, ALU.add))
                chain(dve.tensor_tensor(tab[:, :, :], es[:, 0, :].unsqueeze(2).to_broadcast([1, NSLOT, NE]),
                                        cst[0:1, C_IOTA:C_IOTA + NE].unsqueeze(1).to_broadcast([1, NSLOT, NE]), ALU.is_equal))
                chain(dve.tensor_tensor(tab2[:, :, :], tab[:, :, :], ns[0:1, 3, :].unsqueeze(1).to_broadcast([1, NSLOT, NE]), ALU.mult))
                chain(dve.tensor_reduce(es[:, 1, :], tab2[:, :, :], AX.X, ALU.add))
                chain(dve.tensor_scalar(es[:, 2, :], es[:, 0, :], float(NE), None, ALU.is_lt))
                chain(dve.scalar_tensor_tensor(out=es[:, 3, :], in0=slots, scalar=float(P), in1=es[:, 1, :], op0=ALU.mult, op1=ALU.add))
                chain(dve.tensor_tensor(es[:, 3, :], es[:, 3, :], es[:, 2, :], ALU.mult))
                chain(dve.tensor_scalar(es[:, 2, :], es[:, 2, :], -float(DUMMY_ROW), float(DUMMY_ROW), ALU.mult, ALU.add))
                chain(dve.tensor_tensor(slot_tab[:, 1, :], es[:, 3, :], es[:, 2, :], ALU.add))
                dve.tensor_scalar(slot_tab[:, 0, :], es[:, 0, :], float(NE - 1), None, ALU.min).then_inc(s_tb, 1)

            @block.tensor
            def _(pe):
                pe.wait_ge(s_wl, 48)
                pe.wait_ge(s_pre, 4)

                def emit(n):
                    T = n + -1
                    if T.within(NT):
                        r = T.ring(R)
                        wait(pe, s_z, T, 1, 1)
                        wait(pe, s_zt, T, 1, 0)
                        for c in range(DC):
                            mm = pe.transpose(ps_z[:, c * P:(c + 1) * P], z[:, r, c * P:(c + 1) * P], ident)
                        mm.then_inc(s_tz, 1)
                    T = n + 2
                    if T.within(NT):
                        r = T.ring(R)
                        wait_dma(pe, s_in, T, 2)
                        wait(pe, s_ot, T, 1, -1)
                        for c in range(DC):
                            mm = pe.transpose(ps_o[r % 2][:, c * P:(c + 1) * P], ot[:, r, c * P:(c + 1) * P], ident)
                        mm.then_inc(s_to, 1)
                    T = n + -1
                    if T.within(NT):
                        r = T.ring(R)
                        wait(pe, s_zt, T, 1, 1)
                        wait(pe, s_hot, T, 1, -1)
                        for c in range(DC):
                            mm = pe.matmul(ps_a[r % 2][:, :], zT[:, r, c, :], ct[:, c, :], start=(c == 0), stop=(c == DC - 1))
                        mm.then_inc(s_af, 1)
                    T = n + 1
                    if T.within(NT):
                        r = T.ring(R)
                        wait(pe, s_ot, T, 1, 1)
                        wait(pe, s_x2, T, 1, -1)
                        for c in range(DC):
                            mm = pe.matmul(ps_p[r % 2][:, :], oT[:, r, c, :], wp[:, c, :], start=(c == 0), stop=(c == DC - 1))
                        mm.then_inc(s_pj, 1)
                    T = n + -2
                    if T.within(NT):
                        r = T.ring(R)
                        wait(pe, s_hot, T, 1, 1)
                        wait(pe, s_sn, T, 1, 0)
                        pe.matmul(ps_k[:, 0, :], lt[:, 0, :], hot[:, r, :], start=True, stop=True)
                        pe.matmul(ps_k[:, 1, :], lt[:, 1, :], hot[:, r, :], start=True, stop=True).then_inc(s_rk, 1)

                steps(pe, emit)


def phase_ffn(nc, cols, b2, pay_d, arena, ident, slot_tab, s_w, out, gate):
    with ExitStack() as ctx:
        def sb(name, shape, dt=F32):
            return ctx.enter_context(nc.sbuf_tensor("D_" + name, shape, dt))

        def ps(name, shape, dt=F32):
            return ctx.enter_context(nc.psum_tensor("D_" + name, shape, dt))

        def sem(name):
            return ctx.enter_context(nc.semaphore("D_" + name))

        col = sb("col", [P, NE, 2 * DC + FC])
        b2r = sb("b2r", [P, NE * DIM])
        zz = sb("zz", [P, 2, DIM])
        xT = sb("xT", [P, DC, P])
        hs = sb("hs", [P, FF])
        hr = sb("hr", [P, FC, P])
        tail = sb("tail", [P, 2, DIM + 2])
        al = sb("al", [P, 2, 3])
        y = sb("y", [P, DIM])
        res = sb("res", [P, 2, DIM])
        ps_x = ps("ps_x", [P, DC, P])
        ps_h = [ps(f"ps_h{i}", [P, FF // 2]) for i in range(2)]
        ps_t = [ps(f"ps_t{i}", [P, FC // 2, P]) for i in range(2)]
        ps_y = ps("ps_y", [P, DIM])

        s_wl = sem("small_loaded")
        s_zl = [sem(f"zz_loaded{i}") for i in range(2)]
        s_tl = [sem(f"tail_loaded{i}") for i in range(2)]
        s_tx = sem("zz_transposed")
        s_xt = sem("xT_ready")
        s_m1 = sem("hidden")
        s_h = [sem(f"hidden_copied{i}") for i in range(2)]
        s_th = sem("hidden_transposed")
        s_r = [sem(f"relu{i}") for i in range(2)]
        s_m2 = sem("outputs")
        s_ex = sem("exp")
        s_a = sem("alpha_chain")
        s_y = sem("y")
        s_res = sem("result")
        s_out = [sem(f"out_stored{i}") for i in range(2)]

        def steps(eng, emit):
            run_steps(eng, emit, -1, 4, NSLOT - 3, NSLOT + 1, 2)

        def expert(eng, S):
            return eng.value_load(slot_tab[0:1, 0, bass.ds(S.value(), 1)], min_val=0, max_val=NE - 1)

        with nc.Block() as block:
            @block.sync
            def _(sp):
                sp.dma_start(col[:, :, :], cols).then_inc(s_wl, 16)
                sp.dma_start(b2r[:, :], b2.partition_broadcast(P)).then_inc(s_wl, 16)

                def row(S):
                    return sp.value_load(slot_tab[0:1, 1, bass.ds(S.value(), 1)], min_val=0, max_val=DUMMY_ROW)

                def load_zz(S):
                    if S.within(NSLOT):
                        at = row(S)
                        wait(sp, s_tx, S, 1, -1, alone=gate)
                        sp.dma_start(zz[:, S.ring(2), :], pay_d[bass.ds(at, P), 0:DIM]).then_inc(s_zl[S.ring(2)], 16)

                load_zz(Step(0))

                def emit(n):
                    load_zz(n + 2)
                    S = n
                    if S.within(NSLOT):
                        at = row(S)
                        if S.reg is not None or S.const >= 2:
                            wait_dma(sp, s_out, S + -2, alone=gate)
                        sp.dma_start(tail[:, S.ring(2), :], pay_d[bass.ds(at, P), DIM:PAYW]).then_inc(s_tl[S.ring(2)], 16)

                steps(sp, emit)

            @block.gpsimd
            def _(pool):
                def emit(n):
                    S = n + -1
                    if S.within(NSLOT):
                        wait(pool, s_res, S, 1, 1, alone=gate)
                        pool.indirect_dma_start(out, bass.IndirectOffsetOnAxis(ap=tail[:, S.ring(2), DIM + 1:DIM + 2].bitcast(U32), axis=0),
                                                res[:, S.ring(2), :], None, bounds_check=NTOK - 1, oob_is_err=False).then_inc(s_out[S.ring(2)], 16)

                steps(pool, emit)
                for i in range(2):
                    pool.wait_ge(s_out[i], 16 * ((NSLOT + 1 - i) // 2))

            @block.scalar
            def _(act):
                act.wait_ge(s_wl, 32)

                def emit(n):
                    S = n
                    if S.within(NSLOT):
                        e = expert(act, S)
                        wait(act, s_m1, S, 1, 1)
                        wait(act, s_th, S, 2, 0)
                        act.activation(hs[:, 0:FF // 2], ps_h[0][:, :], ACT.Copy).then_inc(s_h[0], 1)
                    S = n + 1
                    if S.within(NSLOT):
                        e1 = expert(act, S)
                        wait(act, s_tx, S, 1, 1)
                        for c in range(DC):
                            act.activation(xT[:, c, :], ps_x[:, c, :], ACT.Identity,
                                           bias=col[:, bass.ds(e1, 1), DC + c], scale=col[:, bass.ds(e1, 1), c]).then_inc(s_xt, 1)
                    S = n
                    if S.within(NSLOT):
                        wait(act, s_th, S, 2, 1)
                        wait(act, s_m2, S, 1, 0)
                        for c in range(FC // 2):
                            act.activation(hr[:, c, :], ps_t[0][:, c, :], ACT.Relu,
                                           bias=col[:, bass.ds(e, 1), 2 * DC + c]).then_inc(s_r[0], 1)
                        wait_dma(act, s_tl, S)
                        wait(act, s_res, S, 1, -1)
                        act.activation(al[:, S.ring(2), 0:1], tail[:, S.ring(2), DIM:DIM + 1], ACT.Exp, scale=-1.0).then_inc(s_ex, 1)

                steps(act, emit)

            @block.vector
            def _(dve):
                dve.wait_ge(s_wl, 32)

                def emit(n):
                    S = n
                    if S.within(NSLOT):
                        wait(dve, s_m1, S, 1, 1)
                        wait(dve, s_th, S, 2, 0)
                        dve.tensor_copy(hs[:, FF // 2:FF], ps_h[1][:, :]).then_inc(s_h[1], 1)
                    S = n + -1
                    if S.within(NSLOT):
                        e = expert(dve, S)
                        wait(dve, s_ex, S, 1, 1)
                        dve.tensor_scalar(al[:, S.ring(2), 1:2], al[:, S.ring(2), 0:1], 1.0, None, ALU.add).then_inc(s_a, 1)
                        wait(dve, s_a, S, 2, 1)
                        dve.reciprocal(al[:, S.ring(2), 2:3], al[:, S.ring(2), 1:2]).then_inc(s_a, 1)
                        wait(dve, s_m2, S, 1, 1)
                        dve.tensor_tensor(y[:, :], ps_y[:, :], b2r[:, bass.ds(e * DIM, DIM)], ALU.add).then_inc(s_y, 1)
                        wait(dve, s_y, S, 1, 1)
                        wait(dve, s_a, S, 2, 2)
                        if S.reg is not None or S.const >= 2:
                            wait_dma(dve, s_out, S + -2)
                        dve.scalar_tensor_tensor(out=res[:, S.ring(2), :], in0=y[:, :], scalar=al[:, S.ring(2), 2:3],
                                                 in1=tail[:, S.ring(2), 0:DIM],
                                                 op0=ALU.mult, op1=ALU.add).then_inc(s_res, 1)
                    S = n
                    if S.within(NSLOT):
                        e = expert(dve, S)
                        wait(dve, s_th, S, 2, 2)
                        wait(dve, s_m2, S, 1, 0)
                        for c in range(FC // 2, FC):
                            dve.tensor_scalar(hr[:, c, :], ps_t[1][:, c - FC // 2, :], col[:, bass.ds(e, 1), 2 * DC + c], 0.0,
                                              ALU.add, ALU.max).then_inc(s_r[1], 1)

                steps(dve, emit)

            @block.tensor
            def _(pe):
                def emit(n):
                    S = n
                    if S.within(NSLOT):
                        e = expert(pe, S)
                        wait(pe, s_xt, S, DC, DC)
                        wait(pe, s_h[0], S, 1, 0)
                        wait(pe, s_h[1], S, 1, 0)
                        for half in range(2):
                            for c in range(DC):
                                mm = pe.matmul(ps_h[half][:, :], xT[:, c, :],
                                               arena[:, bass.ds(e * WCOLS + c * FF + half * (FF // 2), FF // 2)],
                                               start=(c == 0), stop=(c == DC - 1))
                        mm.then_inc(s_m1, 1)
                    S = n + -1
                    if S.within(NSLOT):
                        e = expert(pe, S)
                        wait(pe, s_y, S, 1, 0)
                        for c in range(FC):
                            if c % (FC // 2) == 0:
                                wait(pe, s_r[c // (FC // 2)], S, FC // 2, FC // 2)
                            mm = pe.matmul(ps_y[:, :], hr[:, c, :], arena[:, bass.ds(e * WCOLS + DC * FF + c * DIM, DIM)],
                                           start=(c == 0), stop=(c == FC - 1))
                        mm.then_inc(s_m2, 1)
                    S = n + 1
                    if S.within(NSLOT):
                        wait_dma(pe, s_zl, S)
                        wait(pe, s_xt, S, DC, 0)
                        for c in range(DC):
                            mm = pe.transpose(ps_x[:, c, :], zz[:, S.ring(2), c * P:(c + 1) * P], ident)
                        mm.then_inc(s_tx, 1)
                    S = n
                    if S.within(NSLOT):
                        for half in range(2):
                            wait(pe, s_h[half], S, 1, 1)
                            wait(pe, s_r[half], S, FC // 2, 0)
                            for c in range(FC // 2):
                                at = (half * (FC // 2) + c) * P
                                mm = pe.transpose(ps_t[half][:, c, :], hs[:, at:at + P], ident)
                            mm.then_inc(s_th, 1)

                steps(pe, emit)


def kernel(**inputs):
    import numpy as np
    import concourse.bacc as bacc
    from concourse.bass_utils import run_bass_kernel_spmd

    def f32(name):
        return np.ascontiguousarray(inputs["L0_" + name])

    w1 = f32("ffn_w1").reshape(NE, FF, DC, P).transpose(0, 3, 2, 1).reshape(NE, P, DC * FF)
    w2 = f32("ffn_w2").reshape(NE, DIM, FC, P).transpose(0, 3, 2, 1).reshape(NE, P, FC * DIM)

    consts = np.zeros((P, C_END), np.float32)
    p = np.arange(P)
    consts[:, C_ID:C_ID + P] = np.eye(P)
    consts[:, C_MASK + QW - P:C_MASK + QW] = np.where(p[None, :] > p[:, None], np.float32(NEG), np.float32(0))
    consts[:, C_LT:C_LT + P] = p[:, None] < p[None, :]
    consts[:, C_IOTA:C_IOTA + NE] = np.arange(NE)
    consts[:, C_RIOTA:C_RIOTA + NE] = NE - np.arange(NE)
    consts[:, C_IOTAP] = (NTOK + p).astype(np.int32).view(np.float32)
    consts[:, C_BLK:C_BLK + NT] = P * np.arange(NT)
    consts[:, C_SLOT:C_SLOT + NSLOT] = np.arange(NSLOT)
    consts[:, C_ID32:C_ID32 + NT] = (P * np.arange(NT)[None, :] + p[:, None]).astype(np.int32).view(np.float32)
    half = HD // 2
    freqs = (np.float32(1.0) / np.float32(10000.0) ** (np.arange(half, dtype=np.float32) / np.float32(half))).astype(np.float32)
    angles = np.arange(SEQ, dtype=np.float32)[:, None] * freqs[None, :]
    cos, sin = np.cos(angles), np.sin(angles)
    rope = np.concatenate([cos, cos, -sin, sin], axis=1).astype(np.float32)

    def per_feature(name):
        return f32(name).reshape(NE, -1, P).transpose(2, 0, 1)

    arrays = {
        "x": f32("attn_x").reshape(NTOK, DIM),
        "w_qkv": np.ascontiguousarray(f32("attn_qkv_w").T),
        "b_qkv": f32("attn_qkv_b"),
        "w_proj": np.ascontiguousarray(f32("attn_proj_w").T),
        "b_proj": f32("attn_proj_b"),
        "cent": np.ascontiguousarray(f32("ffn_centroids").T),
        "w_exp": np.ascontiguousarray(np.concatenate([w1, w2], axis=2)),
        "cols": np.ascontiguousarray(np.concatenate([per_feature("ffn_ln_g"), per_feature("ffn_ln_b"), per_feature("ffn_b1")], axis=2)),
        "b2": f32("ffn_b2").reshape(NE * DIM),
        "consts": consts,
        "rope": rope,
    }
    nc = bacc.Bacc("TRN2", target_bir_lowering=False, num_devices=1)
    args = [nc.dram_tensor("in_" + k, a.shape, mybir.dt.from_np(a.dtype), kind="ExternalInput").ap() for k, a in arrays.items()]
    out = nc.dram_tensor("out", (NTOK, DIM), F32, kind="ExternalOutput").ap()
    program(nc, *args, out)
    r = run_bass_kernel_spmd(nc, [{"in_" + k: a for k, a in arrays.items()}], core_ids=[0])
    return r.results[0]["out"].reshape(BATCH, SEQ, DIM)
```

```python
import concourse.bass as bass
from concourse import mybir
from contextlib import ExitStack

F32 = mybir.dt.float32
BF16 = mybir.dt.bfloat16
I32 = mybir.dt.int32
U32 = mybir.dt.uint32
ALU = mybir.AluOpType
ACT = mybir.ActivationFunctionType
AX = mybir.AxisListType

P = 128
BATCH, SEQ, DIM = 4, 1024, 256
HEADS, HD = 16, 16
NTOK = BATCH * SEQ
NT = NTOK // P
DC = DIM // P
NE, FF = 8, 1024
FC = FF // P
QH = 4
QB = HEADS // QH
NQ = BATCH * QB
KB = SEQ // P
QW = 512
NSPLIT = 3
SROWS = 6 * HD
RS = 3
RR = 4
MROWS = 3
NEG = -1.0e30
EPS = 1e-5
NSLOT = (NTOK + NE * (P - 1)) // P
REGION = NTOK + P
DUMMY_ROW = NE * REGION
PAYW = 2 * DIM + 2
WCOLS = DC * FF + FC * DIM
EARLY = 5

C_ID, C_MASK, C_LT, C_IOTA, C_RIOTA, C_IOTAP, C_BLK, C_SLOT, C_ID32, C_END = (
    0, 128, 256, 384, 392, 400, 401, 433, 472, 504)


class Step:

    def __init__(self, const, reg=None, unroll=1):
        self.const, self.reg, self.unroll = const, reg, unroll

    def __add__(self, k):
        return Step(self.const + k, self.reg, self.unroll)

    def value(self):
        return self.const if self.reg is None else self.reg * self.unroll + self.const

    def within(self, total):
        return self.reg is not None or 0 <= self.const < total

    def ring(self, n):
        assert self.reg is None or self.unroll % n == 0
        return self.const % n


def run_steps(eng, emit, first, lo, hi, last, unroll):
    for n in range(first, lo):
        emit(Step(n))
    assert (hi - lo) % unroll == 0
    with eng.Fori(0, (hi - lo) // unroll) as reg:
        for u in range(unroll):
            emit(Step(lo + u, reg, unroll))
    for n in range(hi, last):
        emit(Step(n))


def wait(eng, sem, step, per=1, plus=0, alone=None):
    if step.reg is None:
        if per * step.const + plus > 0:
            eng.wait_ge(sem, per * step.const + plus)
    else:
        assert per * step.const + plus > 0
        eng.wait_ge(sem, step.reg * (per * step.unroll) + (per * step.const + plus))
        if alone is not None:
            eng.sem_inc(alone, 1)


def wait_dma(eng, sems, step, count=1, alone=None):
    n = len(sems)
    slot = step.ring(n)
    if step.reg is None:
        eng.wait_ge(sems[slot], 16 * count * (step.const // n + 1))
    else:
        eng.wait_ge(sems[slot], step.reg * (16 * count * step.unroll // n) + 16 * count * (step.const // n + 1))
        if alone is not None:
            eng.sem_inc(alone, 1)


def program(nc, x, w_qkv, b_qkv, w_proj, b_proj, cent, w_exp, cols, b2, consts, rope, out):
    ctx = ExitStack()
    with ctx:
        def sem(name):
            return ctx.enter_context(nc.semaphore(name))

        def dram(name, shape, dt):
            return nc.dram_tensor(name, shape, dt, kind="Internal").ap()

        parts_d = dram("qk_parts", [2, NSPLIT, DIM, NTOK], BF16)
        att_d = dram("attention", [NTOK, DIM], F32)
        pay_d = dram("payload", [DUMMY_ROW + P, PAYW], F32)

        arena = ctx.enter_context(nc.sbuf_tensor("arena", [P, NE * WCOLS], F32))
        late = EARLY * WCOLS
        v_all = arena[:, late:late + NT * DIM].rearrange("p (t n) -> p t n", t=NT)
        spare = late + NT * DIM
        cst = ctx.enter_context(nc.sbuf_tensor("cst", [P, C_END], F32))
        ident = cst[:, C_ID:C_ID + P]
        eps = ctx.enter_context(nc.sbuf_tensor("eps", [P, 1], F32))[:, :]
        slot_tab = ctx.enter_context(nc.sbuf_tensor("slot_tab", [1, 2, NSLOT], I32))
        s_cst = sem("consts_loaded")
        s_w = sem("expert_loaded")
        started = sem("started")
        gate = sem("passed")

        wp = ctx.enter_context(nc.sbuf_tensor("w_proj", [P, DC, DIM], F32))
        bp = ctx.enter_context(nc.sbuf_tensor("b_proj", [P, DIM], F32))
        ct = ctx.enter_context(nc.sbuf_tensor("centroids", [P, DC, NE], F32))
        ot = ctx.enter_context(nc.sbuf_tensor("o_tiles", [P, RR, DIM], F32))
        ost = ctx.enter_context(nc.sbuf_tensor("out_normed", [P, KB, QH * HD], F32))
        s_wl = sem("route_weights_loaded")
        s_o = [sem(f"o_loaded{i}") for i in range(RR)]
        s_os = sem("out_stored")

        def load_o(sp, T):
            sp.dma_start(ot[:, T.ring(RR), :], att_d[bass.ds(T.value() * P, P), :]).then_inc(s_o[T.ring(RR)], 16)

        def load_first(sp):
            sp.dma_start(wp[:, :, :], w_proj.rearrange("(c p) n -> p c n", p=P)).then_inc(s_wl, 16)
            sp.dma_start(bp[:, :], b_proj.partition_broadcast(P)).then_inc(s_wl, 16)
            sp.dma_start(ct[:, :, :], cent.rearrange("(c p) n -> p c n", p=P)).then_inc(s_wl, 16)
            for t in range(RR):
                load_o(sp, Step(t))

        with nc.sbuf_tensor("q_stack", [SROWS + MROWS, RS, QH, SEQ], BF16) as qs, \
                nc.sbuf_tensor("k_stack", [SROWS + MROWS, RS, QH, SEQ], BF16) as ks:
            s_stk = [sem(f"stack_loaded{i}") for i in range(RS)]
            s_st = [s for i in range(2) for s in [sem(f"parts_stored{i}")] * 2]
            phase_project(nc, x, w_qkv, b_qkv, consts, rope, parts_d, arena, v_all, cst, ident, eps,
                          qs, ks, s_stk, s_st, s_cst, started, gate)
            phase_attention(nc, w_exp, s_w, parts_d, att_d, v_all, arena, spare, cst, ident, qs, ks, s_stk, s_st,
                            ost, s_os, load_first, gate)
        col = ctx.enter_context(nc.sbuf_tensor("ffn_columns", [P, NE, 2 * DC + FC], F32))
        b2r = ctx.enter_context(nc.sbuf_tensor("ffn_bias2", [P, NE * DIM], F32))
        phase_route(nc, x, pay_d, w_exp, cols, b2, arena, cst, ident, eps, slot_tab, col, b2r,
                    wp, bp, ct, ot, s_wl, s_o, load_o, s_os, gate)
        phase_ffn(nc, pay_d, arena, ident, slot_tab, col, b2r, out, gate)


def load_stack(sp, Q, qs, ks, parts_d, s_stk):
    r, q = Q.ring(RS), Q.value()
    rows, toks = bass.ds((q % QB) * (QH * HD), QH * HD), bass.ds((q // QB) * SEQ, SEQ)

    def put(stack, at, width, kind, part):
        sp.dma_start(stack[at:at + HD * width:width, r, :, :],
                     parts_d[kind, part, rows, toks].rearrange("(h d) n -> d h n", d=HD)).then_inc(s_stk[r], 16)

    for at, width, qp in ((0, 3, 0), (3 * HD, 2, 1), (5 * HD, 1, 2)):
        for j in range(width):
            put(qs, at + j, width, 0, qp)
            put(ks, at + j, width, 1, j)


def phase_project(nc, x, w_qkv, b_qkv, consts, rope, parts_d, arena, v_all, cst, ident, eps,
                  qs, ks, s_stk, s_st, s_cst, started, gate):
    with ExitStack() as ctx:
        def sb(name, shape, dt=F32):
            return ctx.enter_context(nc.sbuf_tensor("A_" + name, shape, dt))

        def ps(name, shape, dt=F32):
            return ctx.enter_context(nc.psum_tensor("A_" + name, shape, dt))

        def sem(name):
            return ctx.enter_context(nc.semaphore("A_" + name))

        R = 4
        place = [0]

        def early(width):
            at = place[0]
            place[0] += R * width
            assert place[0] <= EARLY * WCOLS
            return arena[:, at:at + R * width].rearrange("p (r n) -> p r n", r=R)

        wq = sb("wq", [P, DC, 3 * DIM])
        bq = sb("bq", [P, 3 * DIM])
        rp = sb("rope_tab", [P, KB, 2 * HD])
        xt = early(DIM)
        z = early(DIM)
        zt = early(DC * P).rearrange("p r (c n) -> p r c n", c=DC)
        qk = early(2 * DIM)
        t2 = early(2 * DIM)
        rot = early(2 * DIM)
        res = early(2 * DIM)
        pt = early(4 * NSPLIT * P // 2).rearrange("p r n -> p (r n)").bitcast(BF16).rearrange(
            "p (c j r n) -> p c j r n", c=4, j=NSPLIT, r=R)
        st = sb("st", [P, R, 6])
        mv = sb("mv", [P, R, 2])
        sd = sb("sd", [P, R, 3])
        ps_z = [ps(f"ps_z{i}", [P, DC * P]) for i in range(2)]
        ps_qk = [ps(f"ps_qk{i}", [P, 2 * DIM]) for i in range(2)]
        ps_v = [ps(f"ps_v{i}", [P, DIM]) for i in range(2)]
        ps_r = [ps(f"ps_r{i}", [P, 4 * P]) for i in range(2)]

        s_x = [sem(f"x_loaded{i}") for i in range(R)]
        s_wl = sem("weights_loaded")
        s_var = sem("variance")
        s_ones = sem("ones_preset")
        s_sd = sem("sqrt")
        s_bs = sem("bn_stats")
        s_rs = sem("reciprocal")
        s_nb = sem("shift")
        s_z = sem("z_ready")
        s_tz = sem("z_transposed")
        s_zt = sem("zt_ready")
        s_mm = sem("projected")
        s_qk = sem("qk_biased")
        s_v = sem("v_biased")
        s_t1 = sem("cos_product")
        s_t2 = sem("sin_product")
        s_rot = sem("rotated")
        s_tr = sem("rotated_transposed")
        s_p1 = sem("part1")
        s_r1 = sem("rest1")
        s_p2 = sem("part2")
        s_p3 = sem("part3")

        def steps(eng, emit):
            run_steps(eng, emit, -3, 7, 27, NT + 4, R)

        with nc.Block() as block:
            @block.sync
            def _(sp):
                sp.dma_start(cst[:, :], consts).then_inc(s_cst, 16)
                sp.dma_start(wq[:, :, :], w_qkv.rearrange("(c p) n -> p c n", p=P)).then_inc(s_wl, 16)
                sp.dma_start(bq[:, :], b_qkv.partition_broadcast(P)).then_inc(s_wl, 16)
                sp.dma_start(rp[:, :, :], rope.rearrange("(t p) n -> p t n", p=P)).then_inc(s_wl, 16)

                def load(T):
                    if T.within(NT):
                        wait(sp, s_z, T, 1, 1 - R, alone=gate)
                        sp.dma_start(xt[:, T.ring(R), :], x[bass.ds(T.value() * P, P), :]).then_inc(s_x[T.ring(R)], 16)

                for k in range(2):
                    load(Step(k))

                def emit(n):
                    load(n + 5)
                    T = n + -4
                    if T.within(NT) and T.ring(2) == 1:
                        wait(sp, s_p3, T, 1, 1, alone=gate)
                        r = T.ring(R)
                        for c in range(4):
                            kind, rows = c // 2, slice((c % 2) * P, (c % 2) * P + P)
                            sp.dma_start(
                                parts_d[kind, :, rows, bass.ds((T + -1).value() * P, 2 * P)].rearrange("j p n -> p j n"),
                                pt[:, c, :, r - 1:r + 1, :].rearrange("p j t n -> p j (t n)")).then_inc(s_st[r], 16)
                    if n.reg is None and n.const == 27:
                        for i in range(R):
                            sp.wait_ge(s_st[i], 64 * (KB // R))
                        load_stack(sp, Step(0), qs, ks, parts_d, s_stk)

                steps(sp, emit)

            @block.scalar
            def _(act):
                act.wait_ge(started, 1)

                def emit(n):
                    T = n + 1
                    if T.within(NT):
                        r = T.ring(R)
                        wait(act, s_tz, T, 1, 1)
                        wait(act, s_mm, T, 1, 1 - R)
                        act.activation(zt[:, r, :, :].rearrange("p c n -> p (c n)"), ps_z[r % 2][:, :], ACT.Copy).then_inc(s_zt, 1)
                    T = n + -4
                    if T.within(NT):
                        r = T.ring(R)
                        wait(act, s_r1, T, 1, 1)
                        act.activation(pt[:, :, 1, r, :], res[:, r, :].rearrange("p (c n) -> p c n", c=4),
                                       ACT.Copy).then_inc(s_p2, 1)
                    T = n + 2
                    if T.within(NT):
                        r = T.ring(R)
                        wait(act, s_nb, T, 1, 1)
                        wait(act, s_tz, T, 1, 1 - R)
                        act.activation(z[:, r, :], xt[:, r, :], ACT.Identity, bias=sd[:, r, 2:3],
                                       scale=sd[:, r, 1:2]).then_inc(s_z, 1)
                    T = n + 3
                    if T.within(NT):
                        r = T.ring(R)
                        wait(act, s_var, T, 1, 1)
                        act.activation(sd[:, r, 0:1], mv[:, r, 1:2], ACT.Sqrt, bias=eps).then_inc(s_sd, 1)
                    T = n + -3
                    if T.within(NT):
                        r = T.ring(R)
                        wait(act, s_tr, T, 1, 1)
                        if T.reg is not None or T.const >= R:
                            wait_dma(act, s_st, T + -R, 4)
                        act.activation(pt[:, :, 0, r, :], ps_r[r % 2][:, :].rearrange("p (c n) -> p c n", c=4),
                                       ACT.Copy).then_inc(s_p1, 1)

                steps(act, emit)

            @block.vector
            def _(dve):
                dve.memset(eps, EPS).then_inc(started, 1)
                dve.wait_ge(s_wl, 48)
                dve.wait_ge(s_cst, 16)

                def emit(n):
                    T = n + -4
                    if T.within(NT):
                        r = T.ring(R)
                        wait(dve, s_p1, T, 1, 1)
                        dve.tensor_tensor(res[:, r, :].rearrange("p (c n) -> p c n", c=4),
                                          ps_r[r % 2][:, :].rearrange("p (c n) -> p c n", c=4),
                                          pt[:, :, 0, r, :], ALU.subtract).then_inc(s_r1, 1)
                    T = n + 2
                    if T.within(NT):
                        r = T.ring(R)
                        wait(dve, s_sd, T, 1, 1)
                        dve.reciprocal(sd[:, r, 1:2], sd[:, r, 0:1]).then_inc(s_rs, 1)
                    T = n + -1
                    if T.within(NT):
                        r = T.ring(R)
                        wait(dve, s_mm, T, 1, 1)
                        wait(dve, s_rot, T, 1, 1 - R)
                        dve.tensor_tensor(qk[:, r, :], ps_qk[r % 2][:, :], bq[:, 0:2 * DIM], ALU.add).then_inc(s_qk, 1)
                    T = n + 2
                    if T.within(NT):
                        r = T.ring(R)
                        wait(dve, s_rs, T, 1, 1)
                        dve.scalar_tensor_tensor(out=sd[:, r, 2:3], in0=mv[:, r, 0:1], scalar=-1.0, in1=sd[:, r, 1:2],
                                                 op0=ALU.mult, op1=ALU.mult).then_inc(s_nb, 1)
                    T = n + 3
                    if T.within(NT):
                        r = T.ring(R)
                        wait_dma(dve, s_x, T)
                        dve.bn_stats(st[:, r, :], xt[:, r, :]).then_inc(s_bs, 1)
                    T = n + -1
                    if T.within(NT):
                        r = T.ring(R)
                        dve.tensor_tensor(v_all[:, bass.ds(T.value(), 1), :].rearrange("p a n -> p (a n)"),
                                          ps_v[r % 2][:, :], bq[:, 2 * DIM:3 * DIM], ALU.add).then_inc(s_v, 1)
                    T = n + 3
                    if T.within(NT):
                        r = T.ring(R)
                        wait(dve, s_bs, T, 1, 1, alone=gate)
                        dve.bn_aggr(mv[:, r, :], st[:, r, :]).then_inc(s_var, 1)
                    T = n + -2
                    if T.within(NT):
                        r = T.ring(R)
                        wait(dve, s_t1, T, 1, 1)
                        wait(dve, s_t2, T, 2, 2)
                        dve.tensor_tensor(rot[:, r, :], rot[:, r, :], t2[:, r, :], ALU.add).then_inc(s_rot, 1)
                    T = n + -1
                    if T.within(NT):
                        r = T.ring(R)
                        cos = rp[:, bass.ds(T.value() % KB, 1), 0:HD].to_broadcast([P, 2 * HEADS, HD])
                        wait(dve, s_qk, T, 1, 1)
                        wait(dve, s_tr, T, 1, 1 - R)
                        dve.tensor_tensor(rot[:, r, :].rearrange("p (h d) -> p h d", d=HD),
                                          qk[:, r, :].rearrange("p (h d) -> p h d", d=HD), cos, ALU.mult).then_inc(s_t1, 1)

                steps(dve, emit)

            @block.gpsimd
            def _(pool):
                pool.memset(ks[SROWS:SROWS + MROWS, :, :, :], 1.0).then_inc(s_ones, 1)
                pool.wait_ge(s_ones, 1)

                def emit(n):
                    T = n + -1
                    if T.within(NT):
                        r = T.ring(R)
                        wait(pool, s_qk, T, 1, 1, alone=gate)
                        wait(pool, s_rot, T, 1, 1 - R, alone=gate)
                        src = qk[:, r, :].rearrange("p (h s d) -> p h s d", s=2, d=HD // 2)
                        dst = t2[:, r, :].rearrange("p (h s d) -> p h s d", s=2, d=HD // 2)
                        for s in range(2):
                            sin = rp[:, bass.ds(T.value() % KB, 1), HD + s * HD // 2:HD + (s + 1) * HD // 2]
                            pool.tensor_tensor(dst[:, :, s, :], src[:, :, 1 - s, :],
                                               sin.to_broadcast([P, 2 * HEADS, HD // 2]), ALU.mult).then_inc(s_t2, 1)
                    T = n + -4
                    if T.within(NT):
                        r = T.ring(R)
                        wait(pool, s_p2, T, 1, 1, alone=gate)
                        pool.tensor_tensor(pt[:, :, 2, r, :], res[:, r, :].rearrange("p (c n) -> p c n", c=4),
                                           pt[:, :, 1, r, :], ALU.subtract).then_inc(s_p3, 1)

                steps(pool, emit)

            @block.tensor
            def _(pe):
                pe.wait_ge(s_cst, 16)
                pe.wait_ge(s_wl, 48)

                def emit(n):
                    T = n + 1
                    if T.within(NT):
                        r = T.ring(R)
                        wait(pe, s_z, T, 1, 1)
                        wait(pe, s_zt, T, 1, -1)
                        for c in range(DC):
                            mm = pe.transpose(ps_z[r % 2][:, c * P:(c + 1) * P], z[:, r, c * P:(c + 1) * P], ident)
                        mm.then_inc(s_tz, 1)
                    T = n + -3
                    if T.within(NT):
                        r = T.ring(R)
                        wait(pe, s_rot, T, 1, 1)
                        wait(pe, s_r1, T, 1, -1)
                        for c in range(4):
                            mm = pe.transpose(ps_r[r % 2][:, c * P:(c + 1) * P], rot[:, r, c * P:(c + 1) * P], ident)
                        mm.then_inc(s_tr, 1)
                    T = n
                    if T.within(NT):
                        r = T.ring(R)
                        wait(pe, s_zt, T, 1, 1)
                        wait(pe, s_qk, T, 1, -1)
                        for c in range(DC):
                            pe.matmul(ps_qk[r % 2][:, :], zt[:, r, c, :], wq[:, c, 0:2 * DIM], start=(c == 0), stop=(c == DC - 1))
                        wait(pe, s_v, T, 1, -1)
                        for c in range(DC):
                            mm = pe.matmul(ps_v[r % 2][:, :], zt[:, r, c, :], wq[:, c, 2 * DIM:3 * DIM], start=(c == 0), stop=(c == DC - 1))
                        mm.then_inc(s_mm, 1)

                steps(pe, emit)


def phase_attention(nc, w_exp, s_w, parts_d, att_d, v_all, arena, spare, cst, ident, qs, ks, s_stk, s_st,
                    ost, s_os, load_first, gate):
    with ExitStack() as ctx:
        def sb(name, shape, dt=F32):
            return ctx.enter_context(nc.sbuf_tensor("B_" + name, shape, dt))

        def ps(name, shape, dt=F32):
            return ctx.enter_context(nc.psum_tensor("B_" + name, shape, dt))

        def sem(name):
            return ctx.enter_context(nc.semaphore("B_" + name))

        R = RS
        SUB = KB + KB // 2
        LATE = 4
        NBLK = KB * (KB + 1) // 2
        scale = float(HD) ** -0.5

        vq = sb("v_quad", [P, R, KB, QH, 32])
        pr = arena[:, spare:spare + 2 * QH * QW].rearrange("p (r h n) -> p r h n", r=2, h=QH)
        idb = sb("ident_bf16", [P, P], BF16)
        tri = sb("mask_bf16", [P, P], BF16)
        bmx = sb("block_max", [P, R, QH, NBLK])
        mx = sb("mx", [P, R, QH * KB])
        nm = sb("nm", [QH * KB, MROWS, P], BF16)
        nr = sb("nr", [QH * KB, P])
        oacc = sb("oacc", [P, 2, QW])
        rec = sb("rec", [P, R, KB * QH])
        ps_s = [ps(f"ps_s{i}", [P, QW]) for i in range(R)]
        ps_i = [ps(f"ps_item{i}", [P, 2, QW]) for i in range(2)]
        ps_o = ps("ps_o", [P, QW])

        s_ones = sem("preset")
        s_vone = sem("v_preset")
        s_vq = sem("v_quad")
        s_full = sem("item_written")
        s_free = sem("item_read")
        s_mc = sem("max_combined")
        s_n1 = sem("max_part1")
        s_n2 = sem("max_part2")
        s_n3 = sem("max_part3")
        s_row = sem("max_rows_loaded")
        s_s = sem("scores")
        s_e = sem("exp")
        s_k = sem("masked")
        s_pv = sem("pv")
        s_oe = sem("out_evacuated")
        s_rc = sem("reciprocal")

        subs = [(c, kb, max(0, kb - 4 * c) * P) for c in range(2) for kb in range(4 * c + 4)]
        diag = [i for i, (c, kb, _) in enumerate(subs) if kb >= 4 * c]
        ends = [max(i for i, s in enumerate(subs) if s[0] == c) for c in range(2)]
        assert len(subs) == SUB

        order = (7, 3, 6, 0, 5, 1, 4, 2)
        blocks = [(t, kb) for t in order for kb in range(t + 1)]
        first_block = {t: blocks.index((t, 0)) for t in order}
        assert len(blocks) == NBLK
        banks = []
        for at in range(0, NBLK, 4):
            four = blocks[at:at + 4]
            banks.append([(t, min(kb for u, kb in four if u == t), sum(u == t for u, _ in four),
                           min(x for x in range(4) if four[x][0] == t)) for t in dict.fromkeys(u for u, _ in four)])
        quad_banks = [(h, bank) for h in range(QH) for bank in banks]
        UNITS = len(quad_banks) // 2

        MAXT, OUTT = "maxima transposed", "output transposed"
        queue = iter(range(UNITS))
        plan = []
        for k in range(SUB):
            for slot in range(2):
                if slot == 1 and k % 3 == 2:
                    continue
                plan.append((k, slot, MAXT if (k, slot) == (0, 1) else OUTT if (k, slot) == (7, 0) else next(queue)))
        ITEMS = len(plan)
        assert ITEMS == UNITS + 2 and ITEMS % 2 == 0

        def present(i, item):
            Q = i if item == MAXT else i + -1 if item == OUTT else i + 1
            return Q if Q.within(NQ) else None

        def before(i):
            if i.reg is not None:
                i = Step(1)
            return sum(present(Step(m), e[2]) is not None for m in range(-1, i.const) for e in plan) - ITEMS * i.const

        def number(i, item):
            at = [e[2] for e in plan].index(item)
            return before(i) + sum(present(i, e[2]) is not None for e in plan[:at])

        def buffer(i, item):
            return ps_i[number(i, item) % 2]

        def wait_full(eng, i, item, alone=None):
            wait(eng, s_full, i, ITEMS, number(i, item) + 1, alone)

        def wait_free(eng, i, item, alone=None):
            wait(eng, s_free, i, ITEMS, number(i, item) + 1, alone)

        early_at = (0, 1, 1, 14, 15)
        assert len(early_at) == EARLY

        def sub_at(i, k):
            return (i + -1, k + SUB - LATE) if k < LATE else (i, k - LATE)

        def steps(eng, emit):
            run_steps(eng, emit, -1, 2, 14, NQ + 1, R)

        with nc.Block() as block:
            @block.sync
            def _(sp):
                def load(Q):
                    wait(sp, s_s, Q, QH * SUB, -QH * SUB * (R - 1), alone=gate)
                    load_stack(sp, Q, qs, ks, parts_d, s_stk)

                for s in s_st:
                    sp.wait_ge(s, 64 * (NT // len(s_st)))
                load(Step(1))

                def emit(n):
                    if n.within(NQ):
                        wait(sp, s_n3, n, 1, 1, alone=gate)
                        for j in range(MROWS):
                            sp.dma_start(qs[SROWS + j:SROWS + j + 1, n.ring(R), :, :], nm[:, j, :]).then_inc(s_row, 16)
                    if n.reg is None and n.const == NQ - 1:
                        sp.wait_ge(s_os, 16 * QB)
                        load_first(sp)
                    Q = n + 2
                    if (Q.within(NQ)) and not (Q.reg is None and Q.const < 2):
                        load(Q)
                    Q = n + -1
                    if Q.within(NQ):
                        wait_free(sp, n, OUTT, alone=gate)
                        q = Q.value()
                        sp.dma_start(
                            att_d[bass.ds((q // QB) * SEQ, SEQ), bass.ds((q % QB) * (QH * HD), QH * HD)]
                            .rearrange("(t p) n -> p t n", p=P), ost[:, :, :]).then_inc(s_os, 16)

                steps(sp, emit)

            @block.gpsimd
            def _(pool):
                pool.memset(vq[:, :, :, :, :], 1.0).then_inc(s_vone, 1)
                pool.wait_ge(s_vone, 1)

                def emit(i):
                    if i.reg is None:
                        if i.const == early_at[0]:
                            for s in s_st:
                                pool.wait_ge(s, 64 * (NT // len(s_st)))
                        for e in [e for e in range(EARLY) if early_at[e] == i.const]:
                            pool.dma_start(arena[:, e * WCOLS:(e + 1) * WCOLS], w_exp[e]).then_inc(s_w, 16)
                    Q = i + 1
                    if Q.within(NQ):
                        wait(pool, s_pv, Q, 2 * SUB, -2 * SUB * (R - 1), alone=gate)
                        q = Q.value()
                        pool.tensor_copy(
                            vq[:, Q.ring(R), :, :, 0:HD],
                            v_all[:, bass.ds((q // QB) * KB, KB), bass.ds((q % QB) * (QH * HD), QH * HD)]
                            .rearrange("p t (h d) -> p t h d", h=QH)).then_inc(s_vq, 1)
                    for k in range(SUB):
                        if k == 1 and i.within(NQ):
                            wait_free(pool, i, MAXT, alone=gate)
                            pool.tensor_copy(nm[:, 1, :], nr[:, :]).then_inc(s_n2, 1)
                            wait(pool, s_n2, i, 1, 1, alone=gate)
                            pool.tensor_tensor(nm[:, 2, :], nr[:, :], nm[:, 1, :], ALU.subtract).then_inc(s_n3, 1)
                        Q, s = sub_at(i, k)
                        if Q.within(NQ) and s in diag:
                            for p in range(2):
                                wait(pool, s_e, Q, QH * SUB, QH * s + 2 * p + 2, alone=gate)
                                block_p = pr[:, s % 2, 2 * p:2 * p + 2, 0:P]
                                pool.affine_select(out=block_p, in_=block_p, compare_op=ALU.is_ge, fill=0.0, base=0,
                                                   pattern=[[0, 2], [1, P]], channel_multiplier=-1).then_inc(s_k, 1)

                steps(pool, emit)
                pool.wait_ge(s_w, 16 * EARLY)

            @block.scalar
            def _(act):
                def emit(i):
                    for k in range(SUB):
                        Q, s = sub_at(i, k)
                        if not Q.within(NQ):
                            continue
                        c, kb, off = subs[s]
                        for h in range(QH):
                            if h % 2 == 0:
                                wait(act, s_pv, Q, 2 * SUB, 2 * (s - 2) + h // 2 + 1)
                            wait(act, s_s, Q, QH * SUB, QH * s + h + 1)
                            act.activation(pr[:, s % 2, h, 0:QW - off], ps_s[(QH * s + h) % R][:, 0:QW - off],
                                           ACT.Exp, scale=scale).then_inc(s_e, 1)
                        if s > 0 and s - 1 in ends or s == 0:
                            QE, ce = (Q, 0) if s > 0 else (Q + -1, 1)
                            if QE.within(NQ):
                                evac(QE, ce)
                    if i.reg is None and i.const == NQ:
                        evac(Step(NQ - 1), 1)

                def evac(Q, c):
                    wait(act, s_pv, Q, 2 * SUB, 2 * ends[c] + 2)
                    if present(Q, OUTT) is not None:
                        wait_full(act, Q, OUTT)
                    act.activation(oacc[:, c, :], ps_o[:, :], ACT.Copy).then_inc(s_oe, 1)

                steps(act, emit)

            @block.vector
            def _(dve):
                dve.tensor_copy(idb[:, :], ident).then_inc(s_ones, 1)
                dve.tensor_copy(tri[:, :], cst[:, C_MASK:C_MASK + P]).then_inc(s_ones, 1)

                def emit(i):
                    for k, slot, item in plan:
                        Q = present(i, item)
                        if Q is None:
                            continue
                        src = buffer(i, item)
                        wait_full(dve, i, item, alone=gate if item not in (MAXT, OUTT) else None)
                        if item == MAXT:
                            wait(dve, s_row, i, 16 * MROWS, 0)
                            dve.tensor_scalar(nm[:, 0, :], src[0:QH * KB, 0, 0:P], -1.0, None, ALU.mult).then_inc(s_n1, 1)
                            wait(dve, s_n1, i, 1, 1)
                            dve.scalar_tensor_tensor(out=nr[:, :], in0=src[0:QH * KB, 0, 0:P], scalar=-1.0, in1=nm[:, 0, :],
                                                     op0=ALU.mult, op1=ALU.subtract).then_inc(s_free, 1)
                        elif item == OUTT:
                            view = src[:, :, :].rearrange("p c (g d) -> p (c g) d", d=32)
                            dve.reciprocal(rec[:, Q.ring(R), :], view[:, :, HD]).then_inc(s_rc, 1)
                            wait(dve, s_rc, Q, 1, 1)
                            wait(dve, s_os, Q, 16, 0)
                            dve.tensor_tensor(ost[:, :, :].rearrange("p t (h d) -> p (t h) d", h=QH), view[:, :, 0:HD],
                                              rec[:, Q.ring(R), :].unsqueeze(2).to_broadcast([P, KB * QH, HD]), ALU.mult).then_inc(s_free, 1)
                        else:
                            dve.tensor_reduce(bmx[:, Q.ring(R), :, :].rearrange("p h b -> p (h b)")[:, 8 * item:8 * item + 8],
                                              src[:, :, :].rearrange("p c (b n) -> p (c b) n", n=P),
                                              AX.X, ALU.max).then_inc(s_free, 1)
                            if item == UNITS - 1:
                                wait_free(dve, i, item)
                                for t in range(KB):
                                    dve.tensor_reduce(mx[:, Q.ring(R), :].rearrange("p (h t) -> p h t", h=QH)[:, :, t],
                                                      bmx[:, Q.ring(R), :, first_block[t]:first_block[t] + t + 1],
                                                      AX.X, ALU.max).then_inc(s_mc, 1)

                steps(dve, emit)

            @block.tensor
            def _(pe):
                pe.wait_ge(s_ones, 2)

                def put_item(i, k, slot):
                    for item in [e[2] for e in plan if e[0] == k and e[1] == slot]:
                        Q = present(i, item)
                        if Q is None:
                            continue
                        dst = buffer(i, item)
                        r = Q.ring(R)
                        if item == MAXT:
                            wait(pe, s_mc, Q, KB, KB)
                            wait(pe, s_free, i, ITEMS, number(i, item) - 1)
                            pe.transpose(dst[0:QH * KB, 0, 0:P], mx[:, r, :], ident).then_inc(s_full, 1)
                        elif item == OUTT:
                            wait(pe, s_oe, Q, 2, 2)
                            wait(pe, s_free, i, ITEMS, number(i, item) - 1)
                            for t in range(KB):
                                at = (t % 4) * P
                                mm = pe.transpose(dst[:, t // 4, at:at + P], oacc[:, t // 4, at:at + P], ident)
                            mm.then_inc(s_full, 1)
                        else:
                            if item == 0:
                                wait_dma(pe, s_stk, Q, 12)
                            wait(pe, s_free, i, ITEMS, number(i, item) - 1)
                            for b in range(2):
                                h, bank = quad_banks[2 * item + b]
                                for t, kb, n, at in bank:
                                    masked = kb + n == t + 1
                                    mm = pe.matmul(dst[:, b, at * P:(at + n) * P], qs[0:SROWS, r, h, t * P:(t + 1) * P],
                                                   ks[0:SROWS, r, h, kb * P:(kb + n) * P], start=True, stop=not masked)
                                    if masked:
                                        mm = pe.matmul(dst[:, b, (at + n - 1) * P:(at + n) * P], idb[:, :], tri[:, :],
                                                       start=False, stop=True)
                            mm.then_inc(s_full, 1)

                def scores(Q, s, h):
                    c, kb, off = subs[s]
                    r = Q.ring(R)
                    if s == 0 and h == 0:
                        wait(pe, s_row, Q, 16 * MROWS, 16 * MROWS)
                    wait(pe, s_e, Q, QH * SUB, QH * s + h + 1 - R)
                    pe.matmul(ps_s[(QH * s + h) % R][:, 0:QW - off], ks[:, r, h, kb * P:(kb + 1) * P],
                              qs[:, r, h, c * QW + off:(c + 1) * QW], start=True, stop=True).then_inc(s_s, 1)

                def pv(Q, s, p):
                    c, kb, off = subs[s]
                    r = Q.ring(R)
                    wait(pe, s_e, Q, QH * SUB, QH * s + 2 * p + 2)
                    if s in diag:
                        wait(pe, s_k, Q, 2 * len(diag), 2 * diag.index(s) + p + 1)
                    if s == 0 and p == 0:
                        wait(pe, s_vq, Q, 1, 1)
                    if kb == 0 and p == 0:
                        wait(pe, s_oe, Q, 2, c)
                    for h in (2 * p, 2 * p + 1):
                        mm = pe.matmul(ps_o[32 * h:32 * h + 32, off:QW], vq[:, r, kb, h, :], pr[:, s % 2, h, 0:QW - off],
                                       start=(kb == 0), stop=(kb == 4 * c + 3), tile_position=(0, 32 * h))
                    mm.then_inc(s_pv, 1)

                def emit(i):
                    for k in range(SUB):
                        Q, s = sub_at(i, k)
                        QV, sv = (Q, s - 1) if s > 0 else (Q + -1, SUB - 1)
                        for h in range(QH):
                            if Q.within(NQ):
                                scores(Q, s, h)
                            if h < 2:
                                put_item(i, k, h)
                            elif QV.within(NQ):
                                pv(QV, sv, h - 2)

                steps(pe, emit)


def phase_route(nc, x, pay_d, w_exp, cols, b2, arena, cst, ident, eps, slot_tab, col, b2r,
                wp, bp, ct, ot, s_wl, s_o, load_o_tile, s_os, gate):
    with ExitStack() as ctx:
        def sb(name, shape, dt=F32):
            return ctx.enter_context(nc.sbuf_tensor("C_" + name, shape, dt))

        def ps(name, shape, dt=F32):
            return ctx.enter_context(nc.psum_tensor("C_" + name, shape, dt))

        def sem(name):
            return ctx.enter_context(nc.semaphore("C_" + name))

        R = RR
        xt = sb("xt", [P, R, DIM])
        oT = sb("oT", [P, R, DC, P])
        zT = sb("zT", [P, R, DC, P])
        x2 = sb("x2", [P, R, DIM])
        z = sb("z", [P, R, DIM])
        pay = sb("pay", [P, R, PAYW])
        st = sb("st", [P, R, 2, 6])
        mv = sb("mv", [P, R, 2, 2])
        sd = sb("sd", [P, R, 2, 3])
        top = sb("top", [P, R, 8])
        ge = sb("ge", [P, R, NE])
        pick = sb("pick", [P, R, NE])
        pm = sb("pm", [P, R, 1])
        hot = sb("hot", [P, R, NE], BF16)
        hotf = sb("hotf", [P, R, NE])
        seen = sb("seen", [P, NE])
        rank = sb("rank", [P, R, NE])
        posf = sb("posf", [P, R, 2])
        posi = sb("posi", [P, R, 1], I32)
        lt = sb("lt", [P, 2, P], BF16)
        padrow = sb("padrow", [P, PAYW])
        padidx = sb("padidx", [P, NE], I32)
        cnt = sb("cnt", [P, NE])
        more = sb("more", [P, NE, NT])
        ns = sb("ns", [P, 4, NE])
        tab = sb("tab", [1, NSLOT, NE])
        tab2 = sb("tab2", [1, NSLOT, NE])
        es = sb("es", [1, 4, NSLOT])
        ps_o = [ps(f"ps_o{i}", [P, DC * P]) for i in range(2)]
        ps_p = [ps(f"ps_p{i}", [P, DIM]) for i in range(2)]
        ps_z = ps("ps_z", [P, DC * P])
        ps_a = [ps(f"ps_a{i}", [P, NE]) for i in range(2)]
        ps_k = ps("ps_k", [P, 2, NE])

        s_x = [sem(f"x_loaded{i}") for i in range(R)]
        s_pre = sem("preset")
        s_pad0 = sem("pad_zeroed")
        s_xb = sem("x_biased")
        s_to = sem("o_transposed")
        s_ot = sem("oT_ready")
        s_pj = sem("projected")
        s_x2 = sem("x2")
        s_b1 = sem("bn_stats1")
        s_r1 = sem("reciprocal1")
        s_b2 = sem("bn_stats2")
        s_r2 = sem("reciprocal2")
        s_n1 = sem("shift1")
        s_n2 = sem("shift2")
        s_v1 = sem("var1")
        s_d1 = sem("sqrt1")
        s_z = sem("z_ready")
        s_v2 = sem("var2")
        s_d2 = sem("sqrt2")
        s_zz = sem("zz_ready")
        s_tz = sem("z_transposed")
        s_zt = sem("zT_ready")
        s_af = sem("affinity")
        s_hot = sem("one_hot")
        s_ge, s_rs, s_end = sem("one_hot_chain"), sem("position_chain"), sem("table_chain")
        s_rk = sem("rank_products")
        s_sn = sem("seen")
        s_ps = sem("position")
        s_b = sem("base_ready")
        s_sc = [sem(f"scattered{i}") for i in range(R)]
        s_pi = sem("pad_rows_found")
        s_late = sem("late_expert_loaded")
        s_pad = sem("pads_written")
        s_dum = sem("dummy_rows_written_and_ffn_loaded")

        late_at = [0, 3, 6]
        assert len(late_at) == NE - EARLY

        def steps(eng, emit):
            run_steps(eng, emit, -2, 11, 27, NT + 6, R)

        with nc.Block() as block:
            @block.sync
            def _(sp):
                def load_o(T):
                    if T.within(NT) and (T.reg is not None or T.const >= R):
                        wait(sp, s_to, T, 1, 1 - R, alone=gate)
                        load_o_tile(sp, T)

                def load_x(T):
                    if T.within(NT):
                        r = T.ring(R)
                        wait(sp, s_x2, T, 1, 1 - R, alone=gate)
                        sp.dma_start(xt[:, r, :], x[bass.ds(T.value() * P, P), :]).then_inc(s_x[r], 16)

                load_x(Step(0))
                sp.wait_ge(s_os, 16 * NQ)

                def emit(n):
                    load_o(n + 5)
                    load_x(n + 3)
                    if n.reg is None and n.const in late_at:
                        e = EARLY + late_at.index(n.const)
                        if e > EARLY:
                            sp.wait_ge(s_late, 16 * (e - EARLY))
                        sp.dma_start(arena[:, e * WCOLS:(e + 1) * WCOLS], w_exp[e]).then_inc(s_late, 16)

                steps(sp, emit)
                sp.dma_start(col[:, :, :], cols).then_inc(s_dum, 16)
                sp.dma_start(b2r[:, :], b2.partition_broadcast(P)).then_inc(s_dum, 16)
                sp.wait_ge(s_late, 16 * (NE - EARLY))
                sp.wait_ge(s_pre, 4)
                sp.dma_start(pay_d[DUMMY_ROW:DUMMY_ROW + P, :], padrow[:, :]).then_inc(s_dum, 16)
                sp.wait_ge(s_dum, 48)

            @block.gpsimd
            def _(pool):
                pool.memset(padrow[:, :], 0.0).then_inc(s_pad0, 1)
                pool.wait_ge(s_wl, 48)

                def emit(n):
                    T = n + -6
                    if T.within(NT):
                        r = T.ring(R)
                        wait(pool, s_ps, T, 1, 1, alone=gate)
                        wait(pool, s_zz, T, 1, 1, alone=gate)
                        wait(pool, s_b, T, 2, 2, alone=gate)
                        pool.indirect_dma_start(pay_d[:, :], bass.IndirectOffsetOnAxis(ap=posi[:, r, :].bitcast(U32), axis=0),
                                                pay[:, r, :], None).then_inc(s_sc[r], 16)
                    T = n + 1
                    if T.within(NT):
                        r = T.ring(R)
                        wait_dma(pool, s_x, T, alone=gate)
                        pool.tensor_tensor(xt[:, r, :], xt[:, r, :], bp[:, :], ALU.add).then_inc(s_xb, 1)
                    T = n + -3
                    if T.within(NT):
                        r = T.ring(R)
                        wait(pool, s_z, T, 1, 1, alone=gate)
                        if T.reg is not None or T.const >= R:
                            wait_dma(pool, s_sc, T + -R, alone=gate)
                        pool.tensor_tensor(pay[:, r, DIM:2 * DIM], x2[:, r, :], z[:, r, :], ALU.add).then_inc(s_b, 1)
                        pool.tensor_copy(pay[:, r, 2 * DIM + 1:2 * DIM + 2].bitcast(I32),
                                         cst[:, bass.ds(T.value() + C_ID32, 1)].bitcast(I32)).then_inc(s_b, 1)

                steps(pool, emit)
                pool.wait_ge(s_pi, 1)
                for e in range(NE):
                    pool.indirect_dma_start(pay_d[:, :], bass.IndirectOffsetOnAxis(ap=padidx[:, e:e + 1].bitcast(U32), axis=0),
                                            padrow[:, :], None).then_inc(s_pad, 16)
                pool.wait_ge(s_pad, 16 * NE)
                for i in range(R):
                    pool.wait_ge(s_sc[i], 16 * (NT // R))

            @block.scalar
            def _(act):
                def emit(n):
                    T = n + 2
                    if T.within(NT):
                        r = T.ring(R)
                        wait(act, s_to, T, 1, 1)
                        wait(act, s_pj, T, 1, 1 - R)
                        act.activation(oT[:, r, :, :].rearrange("p c n -> p (c n)"), ps_o[r % 2][:, :], ACT.Copy).then_inc(s_ot, 1)
                    T = n + -2
                    if T.within(NT):
                        r = T.ring(R)
                        wait(act, s_tz, T, 1, 1)
                        wait(act, s_af, T, 1, 1 - R)
                        act.activation(zT[:, r, :, :].rearrange("p c n -> p (c n)"), ps_z[:, :], ACT.Copy).then_inc(s_zt, 1)
                    T = n
                    if T.within(NT):
                        r = T.ring(R)
                        wait(act, s_v1, T, 1, 1)
                        act.activation(sd[:, r, 0, 0:1], mv[:, r, 0, 1:2], ACT.Sqrt, bias=eps).then_inc(s_d1, 1)
                    T = n + -1
                    if T.within(NT):
                        r = T.ring(R)
                        wait(act, s_n1, T, 1, 1)
                        wait(act, s_tz, T, 1, 1 - R)
                        act.activation(z[:, r, :], x2[:, r, :], ACT.Identity, bias=sd[:, r, 0, 2:3],
                                       scale=sd[:, r, 0, 1:2]).then_inc(s_z, 1)
                    T = n + -3
                    if T.within(NT):
                        r = T.ring(R)
                        wait(act, s_n2, T, 1, 1)
                        if T.reg is not None or T.const >= R:
                            wait_dma(act, s_sc, T + -R)
                        act.activation(pay[:, r, 0:DIM], z[:, r, :], ACT.Identity, bias=sd[:, r, 1, 2:3],
                                       scale=sd[:, r, 1, 1:2]).then_inc(s_zz, 1)
                    T = n + -2
                    if T.within(NT):
                        r = T.ring(R)
                        wait(act, s_v2, T, 1, 1)
                        act.activation(sd[:, r, 1, 0:1], mv[:, r, 1, 1:2], ACT.Sqrt, bias=eps).then_inc(s_d2, 1)

                steps(act, emit)

            @block.vector
            def _(dve):
                dve.tensor_copy(lt[:, 0, :], cst[:, C_LT:C_LT + P]).then_inc(s_pre, 1)
                dve.memset(lt[:, 1, :], 1.0).then_inc(s_pre, 1)
                dve.tensor_scalar(seen[:, :], cst[:, C_IOTA:C_IOTA + NE], float(REGION), None, ALU.mult).then_inc(s_pre, 1)
                dve.wait_ge(s_pad0, 1)
                dve.tensor_copy(padrow[:, 2 * DIM + 1:2 * DIM + 2].bitcast(I32),
                                cst[:, C_IOTAP + 0:C_IOTAP + 1].bitcast(I32)).then_inc(s_pre, 1)
                dve.wait_ge(s_wl, 48)

                def emit(n):
                    T = n
                    if T.within(NT):
                        r = T.ring(R)
                        wait(dve, s_pj, T, 1, 1)
                        wait(dve, s_xb, T, 1, 1)
                        wait(dve, s_b, T, 2, -2 * R + 1)
                        dve.tensor_tensor(x2[:, r, :], ps_p[r % 2][:, :], xt[:, r, :], ALU.add).then_inc(s_x2, 1)
                    T = n + -4
                    if T.within(NT):
                        r = T.ring(R)
                        wait(dve, s_af, T, 1, 1)
                        dve.tensor_reduce(top[:, r, 0:1], ps_a[r % 2][:, :], AX.X, ALU.max).then_inc(s_ge, 1)
                    T = n + -1
                    if T.within(NT):
                        r = T.ring(R)
                        wait(dve, s_d1, T, 1, 1)
                        dve.reciprocal(sd[:, r, 0, 1:2], sd[:, r, 0, 0:1]).then_inc(s_r1, 1)
                    T = n
                    if T.within(NT):
                        r = T.ring(R)
                        wait(dve, s_x2, T, 1, 1)
                        dve.bn_stats(st[:, r, 0, :], x2[:, r, :]).then_inc(s_b1, 1)
                    T = n + -4
                    if T.within(NT):
                        r = T.ring(R)
                        wait(dve, s_ge, T, 5, 1)
                        dve.tensor_scalar(ge[:, r, :], ps_a[r % 2][:, :], top[:, r, 0:1], None, ALU.is_ge).then_inc(s_ge, 1)
                    T = n + -1
                    if T.within(NT):
                        r = T.ring(R)
                        wait(dve, s_r1, T, 1, 1)
                        dve.scalar_tensor_tensor(out=sd[:, r, 0, 2:3], in0=mv[:, r, 0, 0:1], scalar=-1.0, in1=sd[:, r, 0, 1:2],
                                                 op0=ALU.mult, op1=ALU.mult).then_inc(s_n1, 1)
                    T = n
                    if T.within(NT):
                        r = T.ring(R)
                        wait(dve, s_b1, T, 1, 1, alone=gate)
                        dve.bn_aggr(mv[:, r, 0, :], st[:, r, 0, :]).then_inc(s_v1, 1)
                    T = n + -4
                    if T.within(NT):
                        r = T.ring(R)
                        wait(dve, s_ge, T, 5, 2)
                        dve.tensor_tensor(pick[:, r, :], ge[:, r, :], cst[:, C_RIOTA:C_RIOTA + NE], ALU.mult).then_inc(s_ge, 1)
                    T = n + -2
                    if T.within(NT):
                        r = T.ring(R)
                        wait(dve, s_z, T, 1, 1)
                        dve.bn_stats(st[:, r, 1, :], z[:, r, :]).then_inc(s_b2, 1)
                    T = n + -4
                    if T.within(NT):
                        r = T.ring(R)
                        wait(dve, s_ge, T, 5, 3)
                        dve.tensor_reduce(pm[:, r, :], pick[:, r, :], AX.X, ALU.max).then_inc(s_ge, 1)
                    T = n + -5
                    if T.within(NT):
                        r = T.ring(R)
                        wait(dve, s_rk, T, 1, 1)
                        wait(dve, s_sn, T, 1, 0)
                        dve.tensor_tensor(rank[:, r, :], ps_k[:, 0, :], seen[:, :], ALU.add).then_inc(s_rs, 1)
                    T = n + -2
                    if T.within(NT):
                        r = T.ring(R)
                        wait(dve, s_b2, T, 1, 1, alone=gate)
                        dve.bn_aggr(mv[:, r, 1, :], st[:, r, 1, :]).then_inc(s_v2, 1)
                    T = n + -4
                    if T.within(NT):
                        r = T.ring(R)
                        wait(dve, s_ge, T, 5, 4)
                        dve.tensor_scalar(hot[:, r, :], cst[:, C_RIOTA:C_RIOTA + NE], pm[:, r, :], None, ALU.is_equal).then_inc(s_hot, 1)
                        dve.tensor_scalar(hotf[:, r, :], cst[:, C_RIOTA:C_RIOTA + NE], pm[:, r, :], None, ALU.is_equal).then_inc(s_ge, 1)
                    T = n + -3
                    if T.within(NT):
                        r = T.ring(R)
                        wait(dve, s_d2, T, 1, 1)
                        dve.reciprocal(sd[:, r, 1, 1:2], sd[:, r, 1, 0:1]).then_inc(s_r2, 1)
                    T = n + -5
                    if T.within(NT):
                        r = T.ring(R)
                        wait(dve, s_rs, T, 3, 1)
                        wait(dve, s_ge, T, 5, 5, alone=gate)
                        dve.tensor_tensor_reduce(pick[:, r, :], rank[:, r, :], hotf[:, r, :], 1.0, 0.0, ALU.mult, ALU.add,
                                                 posf[:, r, 0:1]).then_inc(s_rs, 1)
                        dve.tensor_tensor(seen[:, :], ps_k[:, 1, :], seen[:, :], ALU.add).then_inc(s_sn, 1)
                    T = n + -3
                    if T.within(NT):
                        r = T.ring(R)
                        wait(dve, s_r2, T, 1, 1)
                        dve.scalar_tensor_tensor(out=sd[:, r, 1, 2:3], in0=mv[:, r, 1, 0:1], scalar=-1.0, in1=sd[:, r, 1, 1:2],
                                                 op0=ALU.mult, op1=ALU.mult).then_inc(s_n2, 1)
                    T = n + -5
                    if T.within(NT):
                        r = T.ring(R)
                        wait(dve, s_rs, T, 3, 2)
                        if T.reg is not None or T.const >= R:
                            wait_dma(dve, s_sc, T + -R)
                        dve.tensor_copy(pay[:, r, 2 * DIM:2 * DIM + 1], top[:, r, 0:1]).then_inc(s_rs, 1)
                        dve.tensor_copy(posi[:, r, :], posf[:, r, 0:1]).then_inc(s_ps, 1)

                steps(dve, emit)

                link = [0]

                def chain(ins):
                    link[0] += 1
                    ins.then_inc(s_end, 1)
                    dve.wait_ge(s_end, link[0])

                dve.wait_ge(s_sn, NT)
                chain(dve.tensor_copy(posf[:, 0, 0:1], cst[:, C_IOTAP:C_IOTAP + 1].bitcast(I32)))
                chain(dve.tensor_scalar(posf[:, 0, 1:2], posf[:, 0, 0:1], -float(NTOK), None, ALU.add))
                chain(dve.tensor_scalar(rank[:, 0, :], seen[:, :], posf[:, 0, 1:2], None, ALU.add))
                dve.tensor_copy(padidx[:, :], rank[:, 0, :]).then_inc(s_pi, 1)
                chain(dve.scalar_tensor_tensor(out=cnt[:, :], in0=cst[:, C_IOTA:C_IOTA + NE], scalar=-float(REGION), in1=seen[:, :],
                                               op0=ALU.mult, op1=ALU.add))
                chain(dve.tensor_tensor(more[:, :, :], cnt[:, :].unsqueeze(2).to_broadcast([P, NE, NT]),
                                        cst[:, C_BLK:C_BLK + NT].unsqueeze(1).to_broadcast([P, NE, NT]), ALU.is_gt))
                chain(dve.tensor_reduce(ns[:, 0, :], more[:, :, :], AX.X, ALU.add))
                chain(dve.tensor_copy(ns[:, 1, :], ns[:, 0, :]))
                a, b = 1, 2
                for d in (1, 2, 4):
                    chain(dve.tensor_copy(ns[:, b, 0:d], ns[:, a, 0:d]))
                    chain(dve.tensor_tensor(ns[:, b, d:NE], ns[:, a, d:NE], ns[:, a, 0:NE - d], ALU.add))
                    a, b = b, a
                chain(dve.tensor_tensor(ns[:, 3, :], ns[:, a, :], ns[:, 0, :], ALU.subtract))
                chain(dve.tensor_scalar(ns[:, 3, :], ns[:, 3, :], -float(P), None, ALU.mult))
                chain(dve.scalar_tensor_tensor(out=ns[:, 3, :], in0=cst[:, C_IOTA:C_IOTA + NE], scalar=float(REGION),
                                               in1=ns[:, 3, :], op0=ALU.mult, op1=ALU.add))
                slots = cst[0:1, C_SLOT:C_SLOT + NSLOT]
                by_slot = slots.unsqueeze(2).to_broadcast([1, NSLOT, NE])
                chain(dve.tensor_tensor(tab[:, :, :], by_slot, ns[0:1, a, :].unsqueeze(1).to_broadcast([1, NSLOT, NE]), ALU.is_ge))
                chain(dve.tensor_reduce(es[:, 0, :], tab[:, :, :], AX.X, ALU.add))
                chain(dve.tensor_tensor(tab[:, :, :], es[:, 0, :].unsqueeze(2).to_broadcast([1, NSLOT, NE]),
                                        cst[0:1, C_IOTA:C_IOTA + NE].unsqueeze(1).to_broadcast([1, NSLOT, NE]), ALU.is_equal))
                chain(dve.tensor_tensor(tab2[:, :, :], tab[:, :, :], ns[0:1, 3, :].unsqueeze(1).to_broadcast([1, NSLOT, NE]), ALU.mult))
                chain(dve.tensor_reduce(es[:, 1, :], tab2[:, :, :], AX.X, ALU.add))
                chain(dve.tensor_scalar(es[:, 2, :], es[:, 0, :], float(NE), None, ALU.is_lt))
                chain(dve.scalar_tensor_tensor(out=es[:, 3, :], in0=slots, scalar=float(P), in1=es[:, 1, :], op0=ALU.mult, op1=ALU.add))
                chain(dve.tensor_tensor(es[:, 3, :], es[:, 3, :], es[:, 2, :], ALU.mult))
                chain(dve.tensor_scalar(es[:, 2, :], es[:, 2, :], -float(DUMMY_ROW), float(DUMMY_ROW), ALU.mult, ALU.add))
                chain(dve.tensor_tensor(slot_tab[:, 1, :], es[:, 3, :], es[:, 2, :], ALU.add))
                chain(dve.tensor_scalar(slot_tab[:, 0, :], es[:, 0, :], float(NE - 1), None, ALU.min))

            @block.tensor
            def _(pe):
                pe.wait_ge(s_wl, 48)
                pe.wait_ge(s_pre, 4)

                def emit(n):
                    T = n + 1
                    if T.within(NT):
                        r = T.ring(R)
                        wait(pe, s_ot, T, 1, 1)
                        wait(pe, s_x2, T, 1, -1)
                        for c in range(DC):
                            mm = pe.matmul(ps_p[r % 2][:, :], oT[:, r, c, :], wp[:, c, :], start=(c == 0), stop=(c == DC - 1))
                        mm.then_inc(s_pj, 1)
                    T = n + 2
                    if T.within(NT):
                        r = T.ring(R)
                        wait_dma(pe, s_o, T)
                        wait(pe, s_ot, T, 1, -1)
                        for c in range(DC):
                            mm = pe.transpose(ps_o[r % 2][:, c * P:(c + 1) * P], ot[:, r, c * P:(c + 1) * P], ident)
                        mm.then_inc(s_to, 1)
                    T = n + -2
                    if T.within(NT):
                        r = T.ring(R)
                        wait(pe, s_z, T, 1, 1)
                        wait(pe, s_zt, T, 1, 0)
                        for c in range(DC):
                            mm = pe.transpose(ps_z[:, c * P:(c + 1) * P], z[:, r, c * P:(c + 1) * P], ident)
                        mm.then_inc(s_tz, 1)
                    T = n + -5
                    if T.within(NT):
                        r = T.ring(R)
                        wait(pe, s_hot, T, 1, 1)
                        wait(pe, s_sn, T, 1, 0)
                        pe.matmul(ps_k[:, 0, :], lt[:, 0, :], hot[:, r, :], start=True, stop=True)
                        pe.matmul(ps_k[:, 1, :], lt[:, 1, :], hot[:, r, :], start=True, stop=True).then_inc(s_rk, 1)
                    T = n + -3
                    if T.within(NT):
                        r = T.ring(R)
                        wait(pe, s_zt, T, 1, 1)
                        wait(pe, s_hot, T, 1, -1)
                        for c in range(DC):
                            mm = pe.matmul(ps_a[r % 2][:, :], zT[:, r, c, :], ct[:, c, :], start=(c == 0), stop=(c == DC - 1))
                        mm.then_inc(s_af, 1)

                steps(pe, emit)


def phase_ffn(nc, pay_d, arena, ident, slot_tab, col, b2r, out, gate):
    with ExitStack() as ctx:
        def sb(name, shape, dt=F32):
            return ctx.enter_context(nc.sbuf_tensor("D_" + name, shape, dt))

        def ps(name, shape, dt=F32):
            return ctx.enter_context(nc.psum_tensor("D_" + name, shape, dt))

        def sem(name):
            return ctx.enter_context(nc.semaphore("D_" + name))

        zz = sb("zz", [P, 2, DIM])
        xT = sb("xT", [P, DC, P])
        hs = sb("hs", [P, FF])
        hr = sb("hr", [P, FC, P])
        tail = sb("tail", [P, 2, DIM + 2])
        al = sb("al", [P, 2, 3])
        y = sb("y", [P, DIM])
        res = sb("res", [P, 2, DIM])
        ps_x = ps("ps_x", [P, DC, P])
        ps_h = [ps(f"ps_h{i}", [P, FF // 2]) for i in range(2)]
        ps_t = [ps(f"ps_t{i}", [P, FC // 2, P]) for i in range(2)]
        ps_y = ps("ps_y", [P, DIM])

        s_zl = [sem(f"zz_loaded{i}") for i in range(2)]
        s_tl = [sem(f"tail_loaded{i}") for i in range(2)]
        s_tx = sem("zz_transposed")
        s_xt = sem("xT_ready")
        s_m1 = sem("hidden")
        s_h = [sem(f"hidden_copied{i}") for i in range(2)]
        s_th = sem("hidden_transposed")
        s_r = [sem(f"relu{i}") for i in range(2)]
        s_m2 = sem("outputs")
        s_ex = sem("exp")
        s_a = sem("alpha_chain")
        s_y = sem("y")
        s_res = sem("result")
        s_out = [sem(f"out_stored{i}") for i in range(2)]

        def steps(eng, emit):
            run_steps(eng, emit, -1, 4, NSLOT - 3, NSLOT + 1, 2)

        def expert(eng, S):
            return eng.value_load(slot_tab[0:1, 0, bass.ds(S.value(), 1)], min_val=0, max_val=NE - 1)

        with nc.Block() as block:
            @block.sync
            def _(sp):
                def row(S):
                    return sp.value_load(slot_tab[0:1, 1, bass.ds(S.value(), 1)], min_val=0, max_val=DUMMY_ROW)

                def load_zz(S):
                    if S.within(NSLOT):
                        at = row(S)
                        wait(sp, s_tx, S, 1, -1, alone=gate)
                        sp.dma_start(zz[:, S.ring(2), :], pay_d[bass.ds(at, P), 0:DIM]).then_inc(s_zl[S.ring(2)], 16)

                load_zz(Step(0))

                def emit(n):
                    load_zz(n + 2)
                    S = n
                    if S.within(NSLOT):
                        at = row(S)
                        if S.reg is not None or S.const >= 2:
                            wait_dma(sp, s_out, S + -2, alone=gate)
                        sp.dma_start(tail[:, S.ring(2), :], pay_d[bass.ds(at, P), DIM:PAYW]).then_inc(s_tl[S.ring(2)], 16)

                steps(sp, emit)

            @block.gpsimd
            def _(pool):
                def emit(n):
                    S = n + -1
                    if S.within(NSLOT):
                        wait(pool, s_res, S, 1, 1, alone=gate)
                        pool.indirect_dma_start(out, bass.IndirectOffsetOnAxis(ap=tail[:, S.ring(2), DIM + 1:DIM + 2].bitcast(U32), axis=0),
                                                res[:, S.ring(2), :], None, bounds_check=NTOK - 1, oob_is_err=False).then_inc(s_out[S.ring(2)], 16)

                steps(pool, emit)
                for i in range(2):
                    pool.wait_ge(s_out[i], 16 * ((NSLOT + 1 - i) // 2))

            @block.scalar
            def _(act):
                def emit(n):
                    S = n
                    if S.within(NSLOT):
                        e = expert(act, S)
                        wait(act, s_m1, S, 1, 1)
                        wait(act, s_th, S, 2, 0)
                        act.activation(hs[:, 0:FF // 2], ps_h[0][:, :], ACT.Copy).then_inc(s_h[0], 1)
                    S = n + 1
                    if S.within(NSLOT):
                        e1 = expert(act, S)
                        wait(act, s_tx, S, 1, 1)
                        for c in range(DC):
                            act.activation(xT[:, c, :], ps_x[:, c, :], ACT.Identity,
                                           bias=col[:, bass.ds(e1, 1), DC + c], scale=col[:, bass.ds(e1, 1), c]).then_inc(s_xt, 1)
                    S = n
                    if S.within(NSLOT):
                        wait(act, s_th, S, 2, 1)
                        wait(act, s_m2, S, 1, 0)
                        for c in range(FC // 2):
                            act.activation(hr[:, c, :], ps_t[0][:, c, :], ACT.Relu,
                                           bias=col[:, bass.ds(e, 1), 2 * DC + c]).then_inc(s_r[0], 1)
                        wait_dma(act, s_tl, S)
                        wait(act, s_res, S, 1, -1)
                        act.activation(al[:, S.ring(2), 0:1], tail[:, S.ring(2), DIM:DIM + 1], ACT.Exp, scale=-1.0).then_inc(s_ex, 1)

                steps(act, emit)

            @block.vector
            def _(dve):
                def emit(n):
                    S = n
                    if S.within(NSLOT):
                        wait(dve, s_m1, S, 1, 1)
                        wait(dve, s_th, S, 2, 0)
                        dve.tensor_copy(hs[:, FF // 2:FF], ps_h[1][:, :]).then_inc(s_h[1], 1)
                    S = n + -1
                    if S.within(NSLOT):
                        e = expert(dve, S)
                        wait(dve, s_ex, S, 1, 1)
                        dve.tensor_scalar(al[:, S.ring(2), 1:2], al[:, S.ring(2), 0:1], 1.0, None, ALU.add).then_inc(s_a, 1)
                        wait(dve, s_a, S, 2, 1)
                        dve.reciprocal(al[:, S.ring(2), 2:3], al[:, S.ring(2), 1:2]).then_inc(s_a, 1)
                        wait(dve, s_m2, S, 1, 1)
                        dve.tensor_tensor(y[:, :], ps_y[:, :], b2r[:, bass.ds(e * DIM, DIM)], ALU.add).then_inc(s_y, 1)
                        wait(dve, s_y, S, 1, 1)
                        wait(dve, s_a, S, 2, 2)
                        if S.reg is not None or S.const >= 2:
                            wait_dma(dve, s_out, S + -2)
                        dve.scalar_tensor_tensor(out=res[:, S.ring(2), :], in0=y[:, :], scalar=al[:, S.ring(2), 2:3],
                                                 in1=tail[:, S.ring(2), 0:DIM],
                                                 op0=ALU.mult, op1=ALU.add).then_inc(s_res, 1)
                    S = n
                    if S.within(NSLOT):
                        e = expert(dve, S)
                        wait(dve, s_th, S, 2, 2)
                        wait(dve, s_m2, S, 1, 0)
                        for c in range(FC // 2, FC):
                            dve.tensor_scalar(hr[:, c, :], ps_t[1][:, c - FC // 2, :], col[:, bass.ds(e, 1), 2 * DC + c], 0.0,
                                              ALU.add, ALU.max).then_inc(s_r[1], 1)

                steps(dve, emit)

            @block.tensor
            def _(pe):
                def emit(n):
                    S = n
                    if S.within(NSLOT):
                        e = expert(pe, S)
                        wait(pe, s_xt, S, DC, DC)
                        wait(pe, s_h[0], S, 1, 0)
                        wait(pe, s_h[1], S, 1, 0)
                        for half in range(2):
                            for c in range(DC):
                                mm = pe.matmul(ps_h[half][:, :], xT[:, c, :],
                                               arena[:, bass.ds(e * WCOLS + c * FF + half * (FF // 2), FF // 2)],
                                               start=(c == 0), stop=(c == DC - 1))
                        mm.then_inc(s_m1, 1)
                    S = n + 1
                    if S.within(NSLOT):
                        wait_dma(pe, s_zl, S)
                        wait(pe, s_xt, S, DC, 0)
                        for c in range(DC):
                            mm = pe.transpose(ps_x[:, c, :], zz[:, S.ring(2), c * P:(c + 1) * P], ident)
                        mm.then_inc(s_tx, 1)
                    S = n + -1
                    if S.within(NSLOT):
                        e = expert(pe, S)
                        wait(pe, s_y, S, 1, 0)
                        for c in range(FC):
                            if c % (FC // 2) == 0:
                                wait(pe, s_r[c // (FC // 2)], S, FC // 2, FC // 2)
                            mm = pe.matmul(ps_y[:, :], hr[:, c, :], arena[:, bass.ds(e * WCOLS + DC * FF + c * DIM, DIM)],
                                           start=(c == 0), stop=(c == FC - 1))
                        mm.then_inc(s_m2, 1)
                    S = n
                    if S.within(NSLOT):
                        for half in range(2):
                            wait(pe, s_h[half], S, 1, 1)
                            wait(pe, s_r[half], S, FC // 2, 0)
                            for c in range(FC // 2):
                                at = (half * (FC // 2) + c) * P
                                mm = pe.transpose(ps_t[half][:, c, :], hs[:, at:at + P], ident)
                            mm.then_inc(s_th, 1)

                steps(pe, emit)


def kernel(**inputs):
    import numpy as np
    import concourse.bacc as bacc
    from concourse.bass_utils import run_bass_kernel_spmd

    def f32(name):
        return np.ascontiguousarray(inputs["L0_" + name])

    w1 = f32("ffn_w1").reshape(NE, FF, DC, P).transpose(0, 3, 2, 1).reshape(NE, P, DC * FF)
    w2 = f32("ffn_w2").reshape(NE, DIM, FC, P).transpose(0, 3, 2, 1).reshape(NE, P, FC * DIM)

    consts = np.zeros((P, C_END), np.float32)
    p = np.arange(P)
    consts[:, C_ID:C_ID + P] = np.eye(P)
    consts[:, C_MASK:C_MASK + P] = np.where(p[None, :] > p[:, None], np.float32(NEG), np.float32(0))
    consts[:, C_LT:C_LT + P] = p[:, None] < p[None, :]
    consts[:, C_IOTA:C_IOTA + NE] = np.arange(NE)
    consts[:, C_RIOTA:C_RIOTA + NE] = NE - np.arange(NE)
    consts[:, C_IOTAP] = (NTOK + p).astype(np.int32).view(np.float32)
    consts[:, C_BLK:C_BLK + NT] = P * np.arange(NT)
    consts[:, C_SLOT:C_SLOT + NSLOT] = np.arange(NSLOT)
    consts[:, C_ID32:C_ID32 + NT] = (P * np.arange(NT)[None, :] + p[:, None]).astype(np.int32).view(np.float32)
    half = HD // 2
    freqs = (np.float32(1.0) / np.float32(10000.0) ** (np.arange(half, dtype=np.float32) / np.float32(half))).astype(np.float32)
    angles = np.arange(SEQ, dtype=np.float32)[:, None] * freqs[None, :]
    cos, sin = np.cos(angles), np.sin(angles)
    rope = np.concatenate([cos, cos, -sin, sin], axis=1).astype(np.float32)

    def per_feature(name):
        return f32(name).reshape(NE, -1, P).transpose(2, 0, 1)

    arrays = {
        "x": f32("attn_x").reshape(NTOK, DIM),
        "w_qkv": np.ascontiguousarray(f32("attn_qkv_w").T),
        "b_qkv": f32("attn_qkv_b"),
        "w_proj": np.ascontiguousarray(f32("attn_proj_w").T),
        "b_proj": f32("attn_proj_b"),
        "cent": np.ascontiguousarray(f32("ffn_centroids").T),
        "w_exp": np.ascontiguousarray(np.concatenate([w1, w2], axis=2)),
        "cols": np.ascontiguousarray(np.concatenate([per_feature("ffn_ln_g"), per_feature("ffn_ln_b"), per_feature("ffn_b1")], axis=2)),
        "b2": f32("ffn_b2").reshape(NE * DIM),
        "consts": consts,
        "rope": rope,
    }
    nc = bacc.Bacc("TRN2", target_bir_lowering=False, num_devices=1)
    args = [nc.dram_tensor("in_" + k, a.shape, mybir.dt.from_np(a.dtype), kind="ExternalInput").ap() for k, a in arrays.items()]
    out = nc.dram_tensor("out", (NTOK, DIM), F32, kind="ExternalOutput").ap()
    program(nc, *args, out)
    r = run_bass_kernel_spmd(nc, [{"in_" + k: a for k, a in arrays.items()}], core_ids=[0])
    return r.results[0]["out"].reshape(BATCH, SEQ, DIM)
```
